# Optimizing a Trainium2 kernel written in Bass

```python
import numpy as np
import jax
import jax.numpy as jnp

def _softmax(x, axis=-1):
    return jax.nn.softmax(x, axis=axis)

def _gelu(x):
    return jax.nn.gelu(x, approximate=True)

def _silu(x):
    return jax.nn.silu(x)

def _sigmoid(x):
    return jax.nn.sigmoid(x)

def _layernorm(x, axis=-1, eps=1e-05):
    m = jnp.mean(x, axis=axis, keepdims=True)
    v = jnp.var(x, axis=axis, keepdims=True)
    return (x - m) / jnp.sqrt(v + eps)

def _scatter_add(tgt, idx, src, axis=0):
    return tgt.at[idx].add(src)

def _segment_sum(src, seg, n):
    return jax.ops.segment_sum(src, seg, n)
kernel_name = 'mk_seq_postln_d1_jaxref_r8_47a452'

def setup_inputs(seed: int=0):
    np.random.seed(seed)
    _w = jnp.asarray

    def _L0_attn_setup():
        import jax, jax.numpy as jnp
        import numpy as np
        B, L, HID = (2, 512, 256)
        H, D = (16, HID // 16)
        C = 64
        LOWR = 16
        GLN = 16.0
        EPS = 1e-05

        def _gla_forward(x, Wq, Wk, Wv, Wg1, Wg2, bg2, Wgate, norm_w, Wo):
            Bx, Lx, _ = x.shape
            NC = Lx // C
            scale = D ** (-0.5)

            def heads(y):
                return y.reshape(Bx, Lx, H, D).transpose(0, 2, 1, 3)
            q = heads(x @ Wq)
            k = heads(x @ Wk)
            v = heads(x @ Wv)
            gk = heads(jax.nn.log_sigmoid(x @ Wg1 @ Wg2 + bg2) / GLN)

            def chunked(y):
                return y.reshape(Bx, H, NC, C, D).transpose(2, 0, 1, 3, 4)
            qc, kc, vc = (chunked(q), chunked(k), chunked(v))
            Gc = jnp.cumsum(chunked(gk), axis=3)
            tril = jnp.tril(jnp.ones((C, C), bool))
            S0 = jnp.zeros((Bx, H, D, D), jnp.float32)

            def step(S, inp):
                Q, K, V, G = inp
                Gbase = G[:, :, 0]
                qg = Q * scale * jnp.exp(G)
                o_inter = jnp.einsum('bhld,bhdv->bhlv', qg, S)
                Qh = Q * jnp.exp(G - Gbase[:, :, None]) * scale
                Kh = K * jnp.exp(Gbase[:, :, None] - G)
                A = jnp.einsum('bhld,bhsd->bhls', Qh, Kh)
                A = jnp.where(tril, A, 0.0)
                o_intra = jnp.einsum('bhls,bhsv->bhlv', A, V)
                glast = G[:, :, -1]
                Ks = K * jnp.exp(glast[:, :, None] - G)
                S_new = S * jnp.exp(glast)[..., None] + jnp.einsum('bhld,bhlv->bhdv', Ks, V)
                return (S_new, o_inter + o_intra)
            S_final, o_chunks = jax.lax.scan(step, S0, (qc, kc, vc, Gc))
            o = o_chunks.transpose(1, 3, 0, 2, 4).reshape(Bx, Lx, H, D)
            o = o_chunks.transpose(1, 2, 0, 3, 4).reshape(Bx, H, Lx, D).transpose(0, 2, 1, 3)
            o = o * jax.lax.rsqrt(jnp.mean(o * o, axis=-1, keepdims=True) + EPS) * norm_w
            o = o.reshape(Bx, Lx, HID)
            g = x @ Wgate
            o = o * (g * jax.nn.sigmoid(g))
            return (o @ Wo, S_final)

        def _reference_tuple_inner(x, Wq, Wk, Wv, Wg1, Wg2, bg2, Wgate, norm_w, Wo):
            return _gla_forward(x, Wq, Wk, Wv, Wg1, Wg2, bg2, Wgate, norm_w, Wo)
        key = jax.random.key(seed)
        ks = jax.random.split(key, 10)
        s = lambda fan_in: 1.0 / np.sqrt(fan_in)
        return {'x': jax.random.normal(ks[0], (B, L, HID), jnp.float32), 'Wq': jax.random.normal(ks[1], (HID, HID), jnp.float32) * s(HID), 'Wk': jax.random.normal(ks[2], (HID, HID), jnp.float32) * s(HID), 'Wv': jax.random.normal(ks[3], (HID, HID), jnp.float32) * s(HID), 'Wg1': jax.random.normal(ks[4], (HID, LOWR), jnp.float32) * s(HID), 'Wg2': jax.random.normal(ks[5], (LOWR, HID), jnp.float32) * s(LOWR), 'bg2': jax.random.normal(ks[6], (HID,), jnp.float32) * 0.1, 'Wgate': jax.random.normal(ks[7], (HID, HID), jnp.float32) * s(HID), 'norm_w': jnp.ones((D,), jnp.float32), 'Wo': jax.random.normal(ks[8], (HID, HID), jnp.float32) * s(HID)}
    _L0_attn_in = _L0_attn_setup()

    def _L0_ffn_setup():
        import jax, jax.numpy as jnp
        import numpy as np
        E = 64
        K = 6
        CAP = 64
        SCALE = 1.0
        H = 256
        I = 96
        SI = I * 2
        B, S = (2, 128)

        def _moe(x, gate_w, gate_up_proj, down_proj, shared_gate_w, shared_up_w, shared_down_w):
            b, s, h = x.shape
            T = b * s
            xf = x.reshape(T, h)
            scores = jax.nn.softmax(xf @ gate_w.T, axis=-1)
            topk_w, topk_idx = jax.lax.top_k(scores, K)
            topk_w = topk_w * SCALE
            flat_e = topk_idx.reshape(-1)
            order = jnp.argsort(flat_e)
            sorted_e = flat_e[order]
            sorted_tok = (order // K).astype(jnp.int32)
            sorted_w = topk_w.reshape(-1)[order]
            counts = jnp.zeros((E,), jnp.int32).at[flat_e].add(1)
            offsets = jnp.cumsum(counts) - counts
            pos = jnp.arange(T * K, dtype=jnp.int32) - offsets[sorted_e]
            buf_tok = jnp.full((E, CAP), T, jnp.int32).at[sorted_e, pos].set(sorted_tok, mode='drop')
            buf_w = jnp.zeros((E, CAP), x.dtype).at[sorted_e, pos].set(sorted_w, mode='drop')
            xp = jnp.concatenate([xf, jnp.zeros((1, h), x.dtype)], axis=0)
            gx = xp[buf_tok]
            gu = jnp.einsum('ech,ehi->eci', gx, gate_up_proj)
            g, u = jnp.split(gu, 2, axis=-1)
            hid = jax.nn.silu(g) * u
            eo = jnp.einsum('eci,eih->ech', hid, down_proj) * buf_w[..., None]
            routed = jnp.zeros((T + 1, h), x.dtype).at[buf_tok.reshape(-1)].add(eo.reshape(-1, h))[:T]
            shared = jax.nn.silu(xf @ shared_gate_w.T) * (xf @ shared_up_w.T) @ shared_down_w.T
            return (routed + shared).reshape(b, s, h)
        key = jax.random.key(seed)
        ks = jax.random.split(key, 7)
        x = jax.random.normal(ks[0], (B, S, H), jnp.float32)
        gate_w = jax.random.normal(ks[1], (E, H), jnp.float32) * 0.02
        gate_up_proj = jax.random.normal(ks[2], (E, H, 2 * I), jnp.float32) * 0.02
        down_proj = jax.random.normal(ks[3], (E, I, H), jnp.float32) * 0.02
        shared_gate_w = jax.random.normal(ks[4], (SI, H), jnp.float32) * 0.02
        shared_up_w = jax.random.normal(ks[5], (SI, H), jnp.float32) * 0.02
        shared_down_w = jax.random.normal(ks[6], (H, SI), jnp.float32) * 0.02
        return dict(x=x, gate_w=gate_w, gate_up_proj=gate_up_proj, down_proj=down_proj, shared_gate_w=shared_gate_w, shared_up_w=shared_up_w, shared_down_w=shared_down_w)
    _L0_ffn_in = _L0_ffn_setup()
    _d = {'L0_attn_x': _L0_attn_in['x'], 'L0_attn_Wq': _L0_attn_in['Wq'], 'L0_attn_Wk': _L0_attn_in['Wk'], 'L0_attn_Wv': _L0_attn_in['Wv'], 'L0_attn_Wg1': _L0_attn_in['Wg1'], 'L0_attn_Wg2': _L0_attn_in['Wg2'], 'L0_attn_bg2': _L0_attn_in['bg2'], 'L0_attn_Wgate': _L0_attn_in['Wgate'], 'L0_attn_norm_w': _L0_attn_in['norm_w'], 'L0_attn_Wo': _L0_attn_in['Wo'], 'L0_ffn_gate_w': _L0_ffn_in['gate_w'], 'L0_ffn_gate_up_proj': _L0_ffn_in['gate_up_proj'], 'L0_ffn_down_proj': _L0_ffn_in['down_proj'], 'L0_ffn_shared_gate_w': _L0_ffn_in['shared_gate_w'], 'L0_ffn_shared_up_w': _L0_ffn_in['shared_up_w'], 'L0_ffn_shared_down_w': _L0_ffn_in['shared_down_w']}
    _x0 = _d['L0_attn_x']
    _d['L0_attn_x'] = jax.random.normal(jax.random.fold_in(jax.random.key(seed), 1), (2, 512, 256), dtype=_x0.dtype)
    del _x0
    return _d

def reference(L0_attn_x, L0_attn_Wq, L0_attn_Wk, L0_attn_Wv, L0_attn_Wg1, L0_attn_Wg2, L0_attn_bg2, L0_attn_Wgate, L0_attn_norm_w, L0_attn_Wo, L0_ffn_gate_w, L0_ffn_gate_up_proj, L0_ffn_down_proj, L0_ffn_shared_gate_w, L0_ffn_shared_up_w, L0_ffn_shared_down_w):

    def _L0_attn_ref(x, Wq, Wk, Wv, Wg1, Wg2, bg2, Wgate, norm_w, Wo):
        import jax, jax.numpy as jnp
        import numpy as np
        B, L, HID = (2, 512, 256)
        H, D = (16, HID // 16)
        C = 64
        LOWR = 16
        GLN = 16.0
        EPS = 1e-05

        def _gla_forward(x, Wq, Wk, Wv, Wg1, Wg2, bg2, Wgate, norm_w, Wo):
            Bx, Lx, _ = x.shape
            NC = Lx // C
            scale = D ** (-0.5)

            def heads(y):
                return y.reshape(Bx, Lx, H, D).transpose(0, 2, 1, 3)
            q = heads(x @ Wq)
            k = heads(x @ Wk)
            v = heads(x @ Wv)
            gk = heads(jax.nn.log_sigmoid(x @ Wg1 @ Wg2 + bg2) / GLN)

            def chunked(y):
                return y.reshape(Bx, H, NC, C, D).transpose(2, 0, 1, 3, 4)
            qc, kc, vc = (chunked(q), chunked(k), chunked(v))
            Gc = jnp.cumsum(chunked(gk), axis=3)
            tril = jnp.tril(jnp.ones((C, C), bool))
            S0 = jnp.zeros((Bx, H, D, D), jnp.float32)

            def step(S, inp):
                Q, K, V, G = inp
                Gbase = G[:, :, 0]
                qg = Q * scale * jnp.exp(G)
                o_inter = jnp.einsum('bhld,bhdv->bhlv', qg, S)
                Qh = Q * jnp.exp(G - Gbase[:, :, None]) * scale
                Kh = K * jnp.exp(Gbase[:, :, None] - G)
                A = jnp.einsum('bhld,bhsd->bhls', Qh, Kh)
                A = jnp.where(tril, A, 0.0)
                o_intra = jnp.einsum('bhls,bhsv->bhlv', A, V)
                glast = G[:, :, -1]
                Ks = K * jnp.exp(glast[:, :, None] - G)
                S_new = S * jnp.exp(glast)[..., None] + jnp.einsum('bhld,bhlv->bhdv', Ks, V)
                return (S_new, o_inter + o_intra)
            S_final, o_chunks = jax.lax.scan(step, S0, (qc, kc, vc, Gc))
            o = o_chunks.transpose(1, 3, 0, 2, 4).reshape(Bx, Lx, H, D)
            o = o_chunks.transpose(1, 2, 0, 3, 4).reshape(Bx, H, Lx, D).transpose(0, 2, 1, 3)
            o = o * jax.lax.rsqrt(jnp.mean(o * o, axis=-1, keepdims=True) + EPS) * norm_w
            o = o.reshape(Bx, Lx, HID)
            g = x @ Wgate
            o = o * (g * jax.nn.sigmoid(g))
            return (o @ Wo, S_final)

        def _reference_tuple_inner(x, Wq, Wk, Wv, Wg1, Wg2, bg2, Wgate, norm_w, Wo):
            return _gla_forward(x, Wq, Wk, Wv, Wg1, Wg2, bg2, Wgate, norm_w, Wo)
        return _reference_tuple_inner(x, Wq, Wk, Wv, Wg1, Wg2, bg2, Wgate, norm_w, Wo)[0]

    def _L0_ffn_ref(x, gate_w, gate_up_proj, down_proj, shared_gate_w, shared_up_w, shared_down_w):
        import jax, jax.numpy as jnp
        import numpy as np
        E = 64
        K = 6
        CAP = 64
        SCALE = 1.0
        H = 256
        I = 96
        SI = I * 2
        B, S = (2, 128)

        def _moe(x, gate_w, gate_up_proj, down_proj, shared_gate_w, shared_up_w, shared_down_w):
            b, s, h = x.shape
            T = b * s
            xf = x.reshape(T, h)
            scores = jax.nn.softmax(xf @ gate_w.T, axis=-1)
            topk_w, topk_idx = jax.lax.top_k(scores, K)
            topk_w = topk_w * SCALE
            flat_e = topk_idx.reshape(-1)
            order = jnp.argsort(flat_e)
            sorted_e = flat_e[order]
            sorted_tok = (order // K).astype(jnp.int32)
            sorted_w = topk_w.reshape(-1)[order]
            counts = jnp.zeros((E,), jnp.int32).at[flat_e].add(1)
            offsets = jnp.cumsum(counts) - counts
            pos = jnp.arange(T * K, dtype=jnp.int32) - offsets[sorted_e]
            buf_tok = jnp.full((E, CAP), T, jnp.int32).at[sorted_e, pos].set(sorted_tok, mode='drop')
            buf_w = jnp.zeros((E, CAP), x.dtype).at[sorted_e, pos].set(sorted_w, mode='drop')
            xp = jnp.concatenate([xf, jnp.zeros((1, h), x.dtype)], axis=0)
            gx = xp[buf_tok]
            gu = jnp.einsum('ech,ehi->eci', gx, gate_up_proj)
            g, u = jnp.split(gu, 2, axis=-1)
            hid = jax.nn.silu(g) * u
            eo = jnp.einsum('eci,eih->ech', hid, down_proj) * buf_w[..., None]
            routed = jnp.zeros((T + 1, h), x.dtype).at[buf_tok.reshape(-1)].add(eo.reshape(-1, h))[:T]
            shared = jax.nn.silu(xf @ shared_gate_w.T) * (xf @ shared_up_w.T) @ shared_down_w.T
            return (routed + shared).reshape(b, s, h)
        return _moe(x, gate_w, gate_up_proj, down_proj, shared_gate_w, shared_up_w, shared_down_w)
    x = L0_attn_x
    x = _layernorm(x + _L0_attn_ref(x, L0_attn_Wq, L0_attn_Wk, L0_attn_Wv, L0_attn_Wg1, L0_attn_Wg2, L0_attn_bg2, L0_attn_Wgate, L0_attn_norm_w, L0_attn_Wo), axis=-1)
    x = _layernorm(x + _L0_ffn_ref(x, L0_ffn_gate_w, L0_ffn_gate_up_proj, L0_ffn_down_proj, L0_ffn_shared_gate_w, L0_ffn_shared_up_w, L0_ffn_shared_down_w), axis=-1)
    return x

_drawn_inputs = setup_inputs


def setup_inputs(seed=0):
    import zlib

    import numpy as np

    out = dict(_drawn_inputs(seed))
    spreads = {'L0_attn_norm_w': (1.0, 0.2)}
    factors = {'L0_ffn_gate_w': 8.0,
     'L0_ffn_gate_up_proj': 8.0,
     'L0_ffn_down_proj': 8.0,
     'L0_ffn_shared_gate_w': 3.925,
     'L0_ffn_shared_up_w': 3.885,
     'L0_ffn_shared_down_w': 3.876}
    for name, (base, spread) in spreads.items():
        noise = np.random.default_rng([zlib.crc32(name.encode()), seed]).standard_normal(out[name].shape)
        drawn = base * np.exp(spread * noise) if base else spread * noise
        out[name] = jnp.asarray(drawn.astype(out[name].dtype))
    for name, factor in factors.items():
        out[name] = (out[name] * factor).astype(out[name].dtype)
    return out
```

```python
from contextlib import ExitStack

import numpy as np

import concourse.bass as bass
import concourse.mybir as mybir

F32 = mybir.dt.float32
U32 = mybir.dt.uint32
I32 = mybir.dt.int32
ALU = mybir.AluOpType
ACT = mybir.ActivationFunctionType
AX = mybir.AxisListType

P = 128
B, L, HID = 2, 512, 256
T = B * L
NT = T // P
TPB = L // P
KC = HID // P
H, D = 16, 16
C = 64
LOWR = 16
GLN = 16.0
EPS = 1e-5
E, K, CAP = 64, 6, 64
I = 96
SI = 192
SM = SI // I
NP = E // 2
ROW = HID + 3 * K
WCOL, ICOL, DCOL = HID, HID + K, HID + 2 * K
NOWHERE = 8192
RING = 8
GXR = 4

C_ID, C_BLK, C_TRI, C_ONE, C_CAUS, C_SCAN, C_EI, C_D, C_ECOL, C_PAR, C_EPS, C_END = np.cumsum(
    [0, P, P, P, P, C, KC * P, E, NT * K, NP, 2, 1]).tolist()


def constants():
    c = np.zeros((P, C_END), np.float32)
    p = np.arange(P)
    c[:, C_ID:C_ID + P] = np.eye(P)
    c[:, C_BLK:C_BLK + P] = p[:, None] // D == p[None, :] // D
    c[:, C_TRI:C_TRI + P] = p[:, None] < p[None, :]
    c[:, C_ONE:C_ONE + P] = 1.0
    c[:, C_CAUS:C_CAUS + C] = p[:, None] % C <= np.arange(C)[None, :]
    c[:, C_SCAN:C_SCAN + KC * P] = np.arange(KC * P) % C != 0
    c[:, C_EI:C_EI + E] = np.arange(E)
    token = np.arange(NT)[None, :, None] * P + p[:, None, None]
    c[:, C_D:C_D + NT * K] = (token * K + np.arange(K)[None, None, :] - NOWHERE).reshape(P, NT * K)
    c[:, C_ECOL:C_ECOL + NP] = 2 * np.arange(NP)[None, :] + p[:, None] // C
    c[:, C_PAR:C_PAR + 2] = (p[:, None] // D) % 2 == np.arange(2)[None, :]
    c[:, C_EPS] = EPS
    return c


def alive(m, n):
    return not isinstance(m, int) or 0 <= m < n


def slot_count(p, k):
    return (p - k % GXR) * (16 // GXR) + 16


def ring_count(p, r):
    return (p - r) * (32 // RING) + 32


def first(m):
    return isinstance(m, int) and m == 0


def build(nc, consts, x, Wq, Wk, Wv, Wg1, Wg2, bg2, Wgate, norm_w, Wo, gate_w, gup, down, sg_w, su_w, sd_w, out):
    slots = nc.dram_tensor("slot_rows", [E * CAP, ROW], F32, kind="Internal").ap()
    parts = nc.dram_tensor("choice_rows", [T * K, HID], F32, kind="Internal").ap()
    x_rows = x.rearrange("b (t p) h -> (b t) p h", p=P)
    out_rows = out.rearrange("b (t p) h -> (b t) p h", p=P)

    with ExitStack() as ctx:
        def sb(name, shape, dt=F32):
            return ctx.enter_context(nc.sbuf_tensor(name, shape, dt))

        def ps(name, shape):
            return ctx.enter_context(nc.psum_tensor(name, shape, F32))

        def sem(name):
            return ctx.enter_context(nc.semaphore(name))

        cst = sb("cst", [P, C_END])
        ident, blk, tri, ones = (cst[:, a:a + P] for a in (C_ID, C_BLK, C_TRI, C_ONE))
        caus = cst[:, C_CAUS:C_CAUS + C].bitcast(I32)
        scan_keep = cst[:, C_SCAN:C_SCAN + KC * P]
        eiota = cst[:, C_EI:C_EI + E]
        eps_col = cst[:, C_EPS:C_EPS + 1]
        wq, wk, wv, wg, wo = (sb(n, [P, KC, HID]) for n in ("wq", "wk", "wv", "wg", "wo"))
        wg1 = sb("wg1", [P, KC, LOWR])
        wg2 = sb("wg2", [LOWR + 1, HID])
        nw_col = sb("nw_col", [P, 1])
        raw_g = sb("raw_g", [E, HID])
        raw_s = [sb(n, [I, SM, HID]) for n in ("raw_sg", "raw_su")]
        raw_d = sb("raw_d", [P, KC, SI])
        gwT = sb("gwT", [P, KC, E])
        sT = [sb(n, [P, KC, SI]) for n in ("sgT", "suT")]
        sdT = sb("sdT", [I, SM, HID])
        x_all = sb("x_all", [P, NT, HID])
        x_in = [sb(f"x_in{b}", [P, HID]) for b in range(2)]
        xT = [sb(f"xT{b}", [P, KC, P]) for b in range(2)]
        xTd = sb("xTd", [P, KC * 2, 2, C])
        low = [sb(f"low{b}", [LOWR + 1, P]) for b in range(2)]
        Vbd = [sb(f"Vbd{b}", [P, 16, 2 * D]) for b in range(2)]
        Vn = [sb(f"Vn{b}", [P, HID]) for b in range(2)]
        z_abs = sb("z_abs", [P, KC * P])
        z_exp = sb("z_exp", [P, KC * P])
        z_ln = sb("z_ln", [P, KC * P])
        gk = sb("gk", [P, KC * 2, C])
        Dc = sb("Dc", [P, KC * 2, C])
        EQ = sb("EQ", [P, KC * P])
        EK = sb("EK", [P, KC * P])
        fa = sb("fa", [P, KC * 2])
        fb = sb("fb", [P, KC * 2])
        Qh = [sb(f"Qh{b}", [P, KC, P]) for b in range(2)]
        Kh = sb("Kh", [P, KC, P])
        Kbd = sb("Kbd", [P, KC * 2, 2, C])
        Kt = sb("Kt", [P, HID])
        Am = sb("Am", [P, 4, 4, C])
        Tst = [sb(f"Tst{c}", [P, KC, P]) for c in range(2)]
        Ust = sb("Ust", [P, KC, P])
        Smid = sb("Smid", [P, KC, P])
        Sst = sb("Sst", [P, NT + B, KC * P])
        sq = sb("sq", [P, HID])
        eg = sb("eg", [P, HID])
        eg1 = sb("eg1", [P, HID])
        sigm = sb("sigm", [P, HID])
        ms = sb("ms", [P, H])
        ms_ln = sb("ms_ln", [P, H])
        rs = sb("rs", [P, H])
        sgate = sb("sgate", [P, HID])
        on = sb("on", [P, HID])
        of = sb("of", [P, HID])
        oT = sb("oT", [P, KC, P])
        y = sb("y", [P, HID])
        bn6 = sb("bn6", [P, 6])
        mv = sb("mv", [P, 2])
        v_ln = sb("v_ln", [P, 1])
        rstd = sb("rstd", [P, 1])
        x1r = [sb(f"x1r{b}", [P, ROW]) for b in range(2)]
        x1T = sb("x1T", [P, KC, P])
        x1_all = sb("x1_all", [P, NT, HID])
        x1T_all = sb("x1T_all", [P, NT, KC * P])
        lg = sb("lg", [P, E])
        mx8 = sb("mx8", [P, 8])
        ix8 = sb("ix8", [P, 8], U32)
        nmx = sb("nmx", [P, 1])
        e64 = sb("e64", [P, E])
        e8 = sb("e8", [P, 8])
        esum = sb("esum", [P, 1])
        erec = sb("erec", [P, 1])
        oh = sb("oh", [P, K, E])
        sel = sb("sel", [P, E])
        sel_acc = sb("sel_acc", [P, E])
        pm = sb("pm", [P, K, E])
        pos = sb("pos", [P, K])
        over = sb("over", [P, K])
        slot_f = sb("slot_f", [P, K])
        slot_u = [sb(f"slot_u{b}", [P, K], U32) for b in range(2)]
        filler = sb("filler", [P, 2, ROW])
        zeros = sb("zeros", [P, 3 * HID])
        wgu_r = sb("wgu_r", [P, RING, 2 * KC, 2 * I])
        wdn_r = sb("wdn_r", [I, RING, 2, HID])
        gx = sb("gx", [P, GXR, ROW])
        gxT = sb("gxT", [P, 2, KC * P])
        sg = sb("sg", [I, 2, P])
        hid = sb("hid", [I, 2, P])
        junk = sb("junk", [P, K])
        wsel = sb("wsel", [P, GXR])
        dsel = sb("dsel", [P, GXR])
        dest = [sb(f"dest{b}", [P, 1], U32) for b in range(GXR)]
        eo = [sb(f"eo{b}", [P, HID]) for b in range(GXR)]
        sh_g = sb("sh_g", [I, SM, P])
        sh_h = sb("sh_h", [I, SM, P])
        base = sb("base", [P, NT, HID])
        cin = [sb(f"cin{b}", [P, K * HID]) for b in range(2)]
        csum = sb("csum", [P, HID])
        yf = sb("yf", [P, HID])
        bnf = sb("bnf", [P, 6])
        mvf = sb("mvf", [P, 2])
        vf_ln = sb("vf_ln", [P, 1])
        rstdf = sb("rstdf", [P, 1])
        res = [sb(f"res{b}", [P, HID]) for b in range(2)]

        tA, tB, QK, VO = (ps(n, [P, 512]) for n in ("tA", "tB", "QK", "VO"))
        SC = ps("SC", [P, 4, 512])
        OG = VO
        XTb, GUb, DNb = (tA, tB), (QK, VO), (SC[:, 0, :], SC[:, 1, :])

        s = {}
        for n in ("cst w raw xall fill zero pre prefilled wo_ready low1 "
                  "rawT rawE xTp xT lowp low Vp V zp qk absd expd lnd gk Dc ex ab kh qh kbd khTp Kt sc am am0 Pp0 Pp1 T0 T1 U S "
                  "og sq sigm ege eg ms msl rs sgt on of oTp oT Wop y bn mv vl rst x1 x1Tp x1T x1c x1Tc lgp lg mx ix nmx es idx oh "
                  "sel wr cum acc pm pos ov sf slot dtab rec "
                  "xtp xt gu sig hid dn ev wd dsel dest "
                  "sgp sil shh sdp base csum yf bnf mvf vfl rsf res").split():
            s[n] = sem("s_" + n)
        d_xin = [sem(f"d_xin{b}") for b in range(2)]
        d_scat = [sem(f"d_scat{b}") for b in range(2)]
        d_w = [sem(f"d_w{k}") for k in range(RING)]
        d_gx = [sem(f"d_gx{k}") for k in range(GXR)]
        d_put = [sem(f"d_put{k}") for k in range(GXR)]
        d_cin = [sem(f"d_cin{b}") for b in range(2)]
        d_out = [sem(f"d_out{b}") for b in range(2)]
        N_W = 14 * 16
        NRAW = 4 * 16

        def half(m, par, per):
            return (m + (1 if par else 2)) * (per // 2)

        def run_tiles(eng, body):
            for i in range(-1, 2):
                body(i, i % 2)
            with eng.Fori(1, NT // 2 - 1) as h:
                body(h * 2, 0)
                body(h * 2 + 1, 1)
            for i in range(NT - 2, NT + 2):
                body(i, i % 2)

        def run_pairs(eng, body):
            for p in range(RING):
                body(p, p)
            with eng.Fori(1, NP // RING) as r:
                for k in range(RING):
                    body(r * RING + k, k)
            for p in range(NP, NP + 2):
                body(p, p % RING)

        block = ctx.enter_context(nc.Block())

        @block.sync
        def _(sp):
            def load_x(m, par):
                sp.dma_start(x_in[par][:, :], x_rows[m]).then_inc(d_xin[par], 16)

            sp.dma_start(cst[:, :], consts).then_inc(s["cst"], 16)
            load_x(0, 0)
            load_x(1, 1)
            for n, (t, w) in enumerate(((wg1, Wg1), (wv, Wv), (wq, Wq), (wk, Wk))):
                sp.dma_start(t[:, :, :], w.rearrange("(c p) n -> p c n", p=P)).then_inc(s["w"], 16)
            sp.dma_start(wg2[0:LOWR, :], Wg2).then_inc(s["w"], 16)
            sp.dma_start(wg2[LOWR:LOWR + 1, :], bg2.rearrange("(a n) -> a n", a=1)).then_inc(s["w"], 16)
            sp.dma_start(wg[:, :, :], Wgate.rearrange("(c p) n -> p c n", p=P)).then_inc(s["w"], 16)
            sp.dma_start(wo[:, :, :], Wo.rearrange("(c p) n -> p c n", p=P)).then_inc(s["raw"], 16)
            for h in range(P // D):
                sp.dma_start(nw_col[h * D:(h + 1) * D, :], norm_w.rearrange("(d a) -> d a", a=1)).then_inc(s["raw"], 16)
            sp.dma_start(raw_g[:, :], gate_w).then_inc(s["raw"], 16)
            for t, w in zip(raw_s, (sg_w, su_w)):
                sp.dma_start(t[:, :, :], w.rearrange("(m p) n -> p m n", p=I)).then_inc(s["raw"], 16)
            sp.dma_start(raw_d[:, :, :], sd_w.rearrange("(c p) n -> p c n", p=P)).then_inc(s["raw"], 16)
            sp.dma_start(x_all[:, :, :], x_rows.rearrange("t p h -> p t h")).then_inc(s["xall"], 16)

            def more_x(m, par):
                sp.wait_ge(s["xTp"], m - 1)
                load_x(m, par)
            with sp.Fori(1, NT // 2) as h:
                more_x(h * 2, 0)
                more_x(h * 2 + 1, 1)

            def load_weights(q, k):
                sp.dma_start(wgu_r[:, k, :, :], gup[bass.ds(q * 2, 2)].rearrange("e (c p) n -> p (e c) n", p=P))\
                    .then_inc(d_w[k], 16)
                sp.dma_start(wdn_r[:, k, :, :], down[bass.ds(q * 2, 2)].rearrange("e p n -> p e n")).then_inc(d_w[k], 16)

            def load_slots(p, k):
                if not (isinstance(p, int) and p < GXR):
                    sp.wait_ge(s["xtp"], p - GXR + 1)
                    sp.wait_ge(s["dsel"], p - GXR + 1)
                sp.dma_start(gx[:, k, :], slots[bass.ds(p * P, P)]).then_inc(d_gx[k], 16)

            for q in range(RING):
                load_weights(q, q)
            for par in range(2):
                sp.wait_ge(d_scat[par], half(NT - 2 + par, par, K * 16))
            LAG = 5
            for p in range(RING - LAG):
                load_slots(p, p % GXR)
            with sp.Fori(1, NP // RING) as r:
                for k in range(RING):
                    load_slots(r * RING + (k - LAG), (k - LAG) % GXR)
                    sp.wait_ge(s["dn"], r * RING + (k - RING + 1))
                    load_weights(r * RING + k, k)
            for p in range(NP - LAG, NP):
                load_slots(p, p % GXR)

            for k in range(GXR):
                sp.wait_ge(d_put[k], 16 * (NP // GXR))
            def load_parts(m, par):
                if not (isinstance(m, int) and m < 2):
                    sp.wait_ge(s["csum"], m - 1)
                sp.dma_start(cin[par][:, :], parts[bass.ds(m * (P * K), P * K)].rearrange("(p k) h -> p (k h)", k=K))\
                    .then_inc(d_cin[par], 16)

            def store(m, par):
                sp.wait_ge(s["res"], m + 1)
                sp.dma_start(out_rows[bass.ds(m, 1)].rearrange("a p h -> (a p) h"), res[par][:, :]).then_inc(d_out[par], 16)
            load_parts(0, 0)
            load_parts(1, 1)
            with sp.Fori(1, NT // 2) as h:
                for par in range(2):
                    load_parts(h * 2 + par, par)
                    store(h * 2 + (par - 2), par)
            for m in range(NT - 2, NT):
                store(m, m % 2)
            for par in range(2):
                sp.wait_ge(d_out[par], 16 * (NT // 2))

        @block.gpsimd
        def _(pool):
            pool.memset(filler[:, :, :], 0.0).then_inc(s["fill"], 1)
            pool.wait_ge(s["fill"], 1)
            pool.memset(filler[:, :, ICOL:ICOL + K], -1.0).then_inc(s["fill"], 1)
            pool.memset(zeros[:, :], 0.0).then_inc(s["zero"], 1)
            for t in (Sst, sel_acc, Am):
                pool.memset(t[:, :, :] if t is Sst else t[:, :] if t is sel_acc else t[:, :, :, :], 0.0)\
                    .then_inc(s["pre"], 1)
            for b in range(2):
                pool.memset(Vbd[b][:, :, :], 0.0).then_inc(s["pre"], 1)
                pool.memset(low[b][:, :], 1.0).then_inc(s["low1"], 1)

            def keep(m, par):
                pool.wait_ge(s["x1"], m + 1)
                pool.tensor_copy(x1_all[:, bass.ds(m, 1), :].rearrange("p a h -> p (a h)"), x1r[par][:, 0:HID])\
                    .then_inc(s["x1c"], 1)
                pool.wait_ge(s["x1T"], m + 1)
                pool.tensor_copy(x1T_all[:, bass.ds(m, 1), :].rearrange("p a h -> p (a h)"),
                                 x1T[:, :, :].rearrange("p c t -> p (c t)")).then_inc(s["x1Tc"], 1)

            def dispatch(m, par):
                pool.wait_ge(s["slot"], m + 1)
                pool.wait_ge(s["wr"], m + 1)
                pool.nop(nofuse=True)
                for k in range(K):
                    pool.indirect_dma_start(slots, bass.IndirectOffsetOnAxis(ap=slot_u[par][:, k:k + 1], axis=0),
                                            x1r[par][:, :], None, bounds_check=last_slot,
                                            oob_is_err=False).then_inc(d_scat[par], 16)

            def tile_step(i, par):
                if alive(i - 1, NT):
                    keep(i - 1, 1 - par)
                if alive(i - 2, NT):
                    dispatch(i - 2, par)
            last_slot, last_part = pool.to_reg(E * CAP - 1), pool.to_reg(T * K - 1)
            pool.wait_ge(s["prefilled"], 32)
            run_tiles(pool, tile_step)

            def put(p, k):
                if alive(p - 2, NP):
                    q = (k - 2) % GXR
                    pool.wait_ge(s["dest"], p - 1)
                    pool.wait_ge(s["ev"], p - 1)
                    pool.nop(nofuse=True)
                    pool.indirect_dma_start(parts, bass.IndirectOffsetOnAxis(ap=dest[q][:, :], axis=0),
                                            eo[q][:, :], None, bounds_check=last_part, oob_is_err=False)\
                        .then_inc(d_put[q], 16)
            run_pairs(pool, put)

        @block.tensor
        def _(pe):
            def mm(o, a, b, start, stop=True):
                return pe.matmul(o, a, b, start=start, stop=stop, skip_group_check=True)

            pe.wait_ge(s["cst"], 16)
            pe.wait_ge(s["raw"], 16 * 13)
            for c in range(KC):
                last = pe.transpose(SC[:, 0, c * E:(c + 1) * E], raw_g[:, c * P:(c + 1) * P], ident[0:E, 0:E])
            for n in range(2):
                for c in range(KC):
                    for m in range(SM):
                        last = pe.transpose(SC[:, 1 + n, c * SI + m * I:c * SI + (m + 1) * I],
                                            raw_s[n][:, m, c * P:(c + 1) * P], ident[0:I, 0:I])
            for m in range(SM):
                for c in range(KC):
                    last = pe.transpose(SC[0:I, 3, m * HID + c * P:m * HID + (c + 1) * P],
                                        raw_d[:, c, m * I:(m + 1) * I], ident)
            last.then_inc(s["rawT"], 1)

            def t_x(m, par):
                pe.wait_ge(d_xin[par], half(m, par, 16))
                if alive(m - 3, NT):
                    pe.wait_ge(s["y"], m - 2)
                for c in range(KC):
                    last = pe.transpose(tA[:, c * P:(c + 1) * P], x_in[par][:, c * P:(c + 1) * P], ident)
                last.then_inc(s["xTp"], 1)

            def t_k(m, par):
                pe.wait_ge(s["kh"], m + 1)
                if alive(m - 2, NT):
                    pe.wait_ge(s["lg"], m - 1)
                for c in range(KC):
                    last = pe.transpose(tB[:, c * P:(c + 1) * P], Kh[:, c, :], ident)
                last.then_inc(s["khTp"], 1)

            def scores(m, par):
                pe.wait_ge(s["kbd"], m + 1)
                pe.wait_ge(s["qh"], m + 1)
                if first(m):
                    pe.wait_ge(s["rawE"], 4)
                if alive(m - 1, NT):
                    pe.wait_ge(s["S"], 2 * m)
                if alive(m - 2, NT):
                    pe.wait_ge(s["x1T"], m - 1)
                if alive(m - 3, NT):
                    pe.wait_ge(s["pos"], m - 2)
                for c in range(2):
                    for g in range(KC):
                        for j in range(4):
                            r = slice(32 * j, 32 * j + 32)
                            u = 2 * g + c
                            last = mm(SC[:, j, u * C:(u + 1) * C], Kbd[r, u, :, :].rearrange("p a s -> p (a s)"),
                                      Qh[par][r, g, c * C:(c + 1) * C], True)
                last.then_inc(s["sc"], 1)

            def t_o(m, par):
                pe.wait_ge(s["of"], m + 1)
                if alive(m + 2, NT):
                    pe.wait_ge(s["xT"], m + 3)
                for c in range(KC):
                    last = pe.transpose(tA[:, 256 + c * P:256 + (c + 1) * P], of[:, c * P:(c + 1) * P], ident)
                last.then_inc(s["oTp"], 1)

            def project(m, par):
                pe.wait_ge(s["xT"], m + 1)
                if alive(m - 1, NT):
                    pe.wait_ge(s["Kt"], m)
                if first(m):
                    pe.wait_ge(s["w"], 7 * 16)
                for c in range(KC):
                    last = mm(tB[0:LOWR, 0:P], wg1[:, c, :], xT[par][:, c, :], c == 0, c == KC - 1)
                last.then_inc(s["lowp"], 1)
                if alive(m - 2, NT):
                    pe.wait_ge(s["of"], m - 1)
                for a in range(2):
                    for c in range(KC):
                        last = mm(VO[:, a * HID:(a + 1) * HID],
                                  xTd[:, 2 * c + a, :, :].rearrange("p h t -> p (h t)"),
                                  wv[:, c, :], c == 0, c == KC - 1)
                last.then_inc(s["Vp"], 1)
                if alive(m - 1, NT):
                    pe.wait_ge(s["kh"], m)
                    pe.wait_ge(s["qh"], m)
                for w, o in ((wq, 0), (wk, HID)):
                    for g in range(KC):
                        for c in range(KC):
                            last = mm(QK[:, o + g * P:o + (g + 1) * P], w[:, c, g * P:(g + 1) * P],
                                      xT[par][:, c, :], c == 0, c == KC - 1)
                last.then_inc(s["qk"], 1)

            def out_proj(m, par):
                pe.wait_ge(s["oT"], m + 1)
                if first(m):
                    pe.wait_ge(s["wo_ready"], 2)
                for c in range(KC):
                    last = mm(tA[:, 0:HID], oT[:, c, :], wo[:, c, :], c == 0, c == KC - 1)
                last.then_inc(s["Wop"], 1)

            def decay(m, par):
                pe.wait_ge(s["low"], m + 1)
                for g in range(KC):
                    last = mm(tB[:, 256 + g * P:256 + (g + 1) * P], wg2[:, g * P:(g + 1) * P], low[par][:, :], True)
                last.then_inc(s["zp"], 1)

            def state(m, par):
                pe.wait_ge(s["Kt"], m + 1)
                pe.wait_ge(s["V"], m + 1)
                pe.wait_ge(s["am"], m + 1)
                for c in range(2):
                    r = slice(c * C, (c + 1) * C)
                    for g in range(KC):
                        last = mm(SC[:, c, g * P:(g + 1) * P], Kt[r, g * P:(g + 1) * P], Vn[par][r, g * P:(g + 1) * P], True)
                    last.then_inc(s[f"Pp{c}"], 1)

            def t_x1(m, par):
                pe.wait_ge(s["x1"], m + 1)
                if alive(m + 1, NT):
                    pe.wait_ge(s["am"], m + 2)
                for c in range(KC):
                    last = pe.transpose(SC[:, 3, c * P:(c + 1) * P], x1r[par][:, c * P:(c + 1) * P], ident)
                last.then_inc(s["x1Tp"], 1)

            def count(m, par):
                pe.wait_ge(s["sel"], m + 1)
                if alive(m - 1, NT):
                    pe.wait_ge(s["acc"], m)
                if alive(m + 2, NT):
                    pe.wait_ge(s["am"], m + 3)
                mm(SC[:, 2, 0:E], tri, sel[:, :], True, False)
                mm(SC[:, 2, 0:E], ones, sel_acc[:, :], False).then_inc(s["cum"], 1)

            def attend(m, par):
                if alive(m + 1, NT):
                    pe.wait_ge(s["V"], m + 2)
                for c in range(KC):
                    mm(OG[:, HID:2 * HID], xT[par][:, c, :], wg[:, c, :], c == 0, c == KC - 1)
                for c in range(2):
                    for u in range(P // D):
                        g, j = u // 4, u % 4
                        mm(OG[c * C:(c + 1) * C, u * 32:(u + 1) * 32], Am[:, j, 2 * g + c, :],
                           Vbd[par][:, 8 * c + u, :], False, False)
                for c in range(2):
                    pe.wait_ge(s[f"T{c}"], m + 1)
                    for g in range(KC):
                        last = mm(OG[c * C:(c + 1) * C, g * P:(g + 1) * P], Qh[par][:, g, c * C:(c + 1) * C],
                                  Tst[c][:, g, :], False)
                last.then_inc(s["og"], 1)

            def logits(m, par):
                pe.wait_ge(s["x1T"], m + 1)
                if alive(m + 2, NT):
                    pe.wait_ge(s["gk"], m + 3)
                if first(m):
                    pe.wait_ge(s["rawE"], 4)
                for c in range(KC):
                    last = mm(tB[:, 0:E], x1T[:, c, :], gwT[:, c, :], c == 0, c == KC - 1)
                last.then_inc(s["lgp"], 1)

            def tile_step(i, par):
                if alive(i + 1, NT):
                    t_x(i + 1, 1 - par)
                if alive(i, NT):
                    t_k(i, par)
                    scores(i, par)
                if alive(i - 1, NT):
                    t_o(i - 1, 1 - par)
                if alive(i + 1, NT):
                    project(i + 1, 1 - par)
                if alive(i - 1, NT):
                    out_proj(i - 1, 1 - par)
                if alive(i + 1, NT):
                    decay(i + 1, 1 - par)
                if alive(i, NT):
                    state(i, par)
                if alive(i - 1, NT):
                    t_x1(i - 1, 1 - par)
                if alive(i - 2, NT):
                    count(i - 2, par)
                if alive(i, NT):
                    attend(i, par)
                if alive(i - 1, NT):
                    logits(i - 1, 1 - par)
            run_tiles(pe, tile_step)

            def shared(m):
                if first(m):
                    pe.wait_ge(s["pos"], NT)
                    pe.wait_ge(s["x1T"], NT)
                    pe.wait_ge(s["x1Tc"], NT)
                else:
                    pe.wait_ge(s["shh"], m)
                xt = x1T_all[:, bass.ds(m, 1), :]
                for a in range(SM):
                    for n in range(2):
                        for c in range(KC):
                            last = mm(SC[0:I, 2, (2 * a + n) * P:(2 * a + n + 1) * P], sT[n][:, c, a * I:(a + 1) * I],
                                      xt[:, :, c * P:(c + 1) * P].rearrange("p a t -> p (a t)"), c == 0, c == KC - 1)
                last.then_inc(s["sgp"], 1)
                pe.wait_ge(s["shh"], m + 1)
                if not first(m):
                    pe.wait_ge(s["base"], m)
                for a in range(SM):
                    last = mm(SC[:, 3, 0:HID], sh_h[:, a, :], sdT[:, a, :], a == 0, a == SM - 1)
                last.then_inc(s["sdp"], 1)
            shared(0)
            with pe.Fori(1, NT // 2) as m:
                shared(m)

            def pair_step(p, k):
                if alive(p, NP):
                    pe.wait_ge(d_gx[k % GXR], slot_count(p, k))
                    if alive(p - 2, NP):
                        pe.wait_ge(s["xt"], p - 1)
                    for c in range(KC):
                        last = pe.transpose(XTb[k % 2][:, c * P:(c + 1) * P], gx[:, k % GXR, c * P:(c + 1) * P], ident)
                    last.then_inc(s["xtp"], 1)
                if alive(p - 1, NP):
                    q, r = (k - 1) % 2, (k - 1) % RING
                    pe.wait_ge(d_w[r], ring_count(p - 1, r))
                    pe.wait_ge(s["xt"], p)
                    if alive(p - 3, NP):
                        pe.wait_ge(s["hid"], p - 2)
                    for e in range(2):
                        for n in range(2):
                            for c in range(KC):
                                o = (2 * n + e) * CAP
                                last = mm(GUb[q][0:I, o:o + CAP], wgu_r[:, r, 2 * e + c, n * I:(n + 1) * I],
                                          gxT[:, q, c * P + e * CAP:c * P + (e + 1) * CAP], c == 0, c == KC - 1)
                    last.then_inc(s["gu"], 1)
                if alive(p - 2, NP):
                    q, r = k % 2, (k - 2) % RING
                    pe.wait_ge(s["hid"], p - 1)
                    if alive(p - 4, NP):
                        pe.wait_ge(s["ev"], p - 3)
                    for e in range(2):
                        last = mm(DNb[q][e * CAP:(e + 1) * CAP, 0:HID], hid[:, q, e * CAP:(e + 1) * CAP],
                                  wdn_r[:, r, e, :], True)
                    last.then_inc(s["dn"], 1)
            run_pairs(pe, pair_step)
            with pe.Fori(NT // 2, NT) as m:
                shared(m)

        @block.scalar
        def _(act):
            act.wait_ge(s["fill"], 2)
            act.dma_start(slots.rearrange("(p a) n -> p a n", p=P),
                          filler[:, 0:1, :].to_broadcast([P, E * CAP // P, ROW])).then_inc(s["prefilled"], 16)
            act.wait_ge(s["zero"], 1)
            act.dma_start(parts.rearrange("(p a b) n -> p a (b n)", p=P, b=3),
                          zeros[:, :].unsqueeze(1).to_broadcast([P, T * K // P // 3, 3 * HID])).then_inc(s["prefilled"], 16)

            def copy(o, i):
                return act.activation(o, i, ACT.Copy)

            def gate_in(m, par):
                act.wait_ge(s["og"], m + 1)
                act.activation(sq[:, :], OG[:, 0:HID], ACT.Square).then_inc(s["sq"], 1)
                act.activation(eg[:, :], OG[:, HID:2 * HID], ACT.Exp, scale=-1.0).then_inc(s["ege"], 1)
                act.wait_ge(s["ege"], m + 1)
                act.activation(eg1[:, :], eg[:, :], ACT.Identity, bias=ones[:, 0:1]).then_inc(s["eg"], 1)

            def rms(m, par):
                act.wait_ge(s["ms"], m + 1)
                act.activation(ms_ln[:, :], ms[:, :], ACT.Ln, bias=eps_col, scale=1.0 / D).then_inc(s["msl"], 1)
                act.wait_ge(s["msl"], m + 1)
                act.activation(rs[:, :], ms_ln[:, :], ACT.Exp, scale=-0.5).then_inc(s["rs"], 1)

            def ev_x(m, par):
                act.wait_ge(s["xTp"], m + 1)
                copy(xT[par][:, :, :].rearrange("p c t -> p (c t)"), tA[:, 0:256])
                copy(xTd[:, :, :, :], tA[:, 0:256].rearrange("p (u t) -> p u t", t=C).unsqueeze(2)
                     .to_broadcast([P, KC * 2, 2, C])).then_inc(s["xT"], 1)

            def ev_k(m, par):
                act.wait_ge(s["khTp"], m + 1)
                copy(Kt[:, :], tB[:, 0:HID]).then_inc(s["Kt"], 1)

            def ev_o(m, par):
                act.wait_ge(s["oTp"], m + 1)
                copy(oT[:, :, :].rearrange("p c t -> p (c t)"), tA[:, 256:512]).then_inc(s["oT"], 1)

            def ev_low(m, par):
                act.wait_ge(s["lowp"], m + 1)
                copy(low[par][0:LOWR, :], tB[0:LOWR, 0:P]).then_inc(s["low"], 1)

            def ev_v(m, par):
                act.wait_ge(s["Vp"], m + 1)
                v = VO[:, :].rearrange("p (u n) -> p u n", n=2 * D)
                for h in range(2):
                    copy(Vbd[par][h * C:(h + 1) * C, :, h * D:(h + 1) * D], v[h * C:(h + 1) * C, :, h * D:(h + 1) * D])
                for c in range(2):
                    last = copy(Vn[par][c * C:(c + 1) * C, :], VO[c * C:(c + 1) * C, c * HID:(c + 1) * HID])
                last.then_inc(s["V"], 1)

            def soft(m, par):
                act.wait_ge(s["zp"], m + 1)
                act.activation(z_abs[:, :], tB[:, 256:512], ACT.Abs).then_inc(s["absd"], 1)
                act.wait_ge(s["absd"], m + 1)
                act.activation(z_exp[:, :], z_abs[:, :], ACT.Exp, scale=-1.0).then_inc(s["expd"], 1)
                act.wait_ge(s["expd"], m + 1)
                if alive(m - 1, NT):
                    act.wait_ge(s["gk"], m)
                act.activation(z_ln[:, :], z_exp[:, :], ACT.Ln, bias=ones[:, 0:1]).then_inc(s["lnd"], 1)

            def ln_std(m, par):
                act.wait_ge(s["mv"], m + 1)
                act.activation(v_ln[:, :], mv[:, 1:2], ACT.Ln, bias=eps_col).then_inc(s["vl"], 1)
                act.wait_ge(s["vl"], m + 1)
                act.activation(rstd[:, :], v_ln[:, :], ACT.Exp, scale=-0.5).then_inc(s["rst"], 1)

            def decays(m, par):
                act.wait_ge(s["Dc"], m + 1)
                d = Dc[:, :, :].rearrange("p u s -> p (u s)")
                act.activation(EQ[:, :], d, ACT.Exp, scale=1.0 / GLN)
                act.activation(EK[:, :], d, ACT.Exp, scale=-1.0 / GLN).then_inc(s["ex"], 1)
                act.activation(fa[:, :], gk[:, :, 0], ACT.Exp, scale=1.0 / GLN)
                act.activation(fb[:, :], Dc[:, :, C - 1], ACT.Exp, scale=1.0 / GLN).then_inc(s["ab"], 1)

            def ev_x1(m, par):
                act.wait_ge(s["x1Tp"], m + 1)
                if alive(m - 1, NT):
                    act.wait_ge(s["x1Tc"], m)
                copy(x1T[:, :, :].rearrange("p c t -> p (c t)"), SC[:, 3, 0:256]).then_inc(s["x1T"], 1)

            def softmax(m, par):
                act.wait_ge(s["nmx"], m + 1)
                act.activation(e64[:, :], lg[:, :], ACT.Exp, bias=nmx[:, :], accum_out=esum[:, :])
                act.activation(e8[:, :], mx8[:, :], ACT.Exp, bias=nmx[:, :]).then_inc(s["es"], 1)

            act.wait_ge(s["cst"], 16)
            act.wait_ge(s["low1"], 2)
            act.wait_ge(s["pre"], 5)

            def tile_step(i, par):
                if alive(i - 1, NT):
                    gate_in(i - 1, 1 - par)
                if alive(i + 1, NT):
                    ev_x(i + 1, 1 - par)
                if alive(i - 1, NT):
                    rms(i - 1, 1 - par)
                if alive(i, NT):
                    ev_k(i, par)
                if alive(i + 1, NT):
                    ev_low(i + 1, 1 - par)
                if alive(i - 1, NT):
                    ev_o(i - 1, 1 - par)
                if alive(i + 1, NT):
                    ev_v(i + 1, 1 - par)
                    soft(i + 1, 1 - par)
                if alive(i - 1, NT):
                    ln_std(i - 1, 1 - par)
                if alive(i - 1, NT):
                    ev_x1(i - 1, 1 - par)
                if alive(i + 1, NT):
                    decays(i + 1, 1 - par)
                if alive(i - 1, NT):
                    softmax(i - 1, 1 - par)
            run_tiles(act, tile_step)

            def shared(m):
                act.wait_ge(s["sgp"], m + 1)
                g = SC[0:I, 2, :].rearrange("p (a n t) -> p a n t", a=SM, n=2)
                if not first(m):
                    act.wait_ge(s["shh"], m)
                act.activation(sh_g[:, :, :], g[:, :, 0, :], ACT.Silu).then_inc(s["sil"], 1)
            shared(0)
            with act.Fori(1, NT // 2) as m:
                shared(m)

            def pair_step(p, k):
                if alive(p, NP):
                    act.wait_ge(s["xtp"], p + 1)
                    if alive(p - 2, NP):
                        act.wait_ge(s["gu"], p - 1)
                    copy(gxT[:, k % 2, :], XTb[k % 2][:, 0:HID]).then_inc(s["xt"], 1)
                if alive(p - 1, NP):
                    q = (k - 1) % 2
                    act.wait_ge(s["gu"], p)
                    if alive(p - 3, NP):
                        act.wait_ge(s["hid"], p - 2)
                    act.activation(sg[:, q, :], GUb[q][0:I, 0:P], ACT.Silu).then_inc(s["sig"], 1)
                if alive(p - 2, NP):
                    q, r = k % 2, (k - 2) % GXR
                    act.wait_ge(s["dn"], p - 1)
                    act.wait_ge(s["wd"], p - 1)
                    if alive(p - 2 - GXR, NP):
                        act.wait_ge(d_put[r], slot_count(p - 2 - GXR, r))
                    act.activation(eo[r][:, :], DNb[q][:, 0:HID], ACT.Copy, scale=wsel[:, r:r + 1]).then_inc(s["ev"], 1)
            run_pairs(act, pair_step)
            with act.Fori(NT // 2, NT) as m:
                shared(m)

            def final_std(m):
                act.wait_ge(s["mvf"], m + 1)
                act.activation(vf_ln[:, :], mvf[:, 1:2], ACT.Ln, bias=eps_col).then_inc(s["vfl"], 1)
                act.wait_ge(s["vfl"], m + 1)
                act.activation(rstdf[:, :], vf_ln[:, :], ACT.Exp, scale=-0.5).then_inc(s["rsf"], 1)
            with act.Fori(0, NT) as m:
                final_std(m)

        @block.vector
        def _(dve):
            dve.wait_ge(s["cst"], 16)
            dve.wait_ge(s["raw"], 16 * 13)
            for c in range(KC):
                dve.tensor_scalar(wo[:, c, :], wo[:, c, :], nw_col[:, 0:1], None, ALU.mult).then_inc(s["wo_ready"], 1)
            dve.wait_ge(s["rawT"], 1)
            dve.tensor_copy(gwT[:, :, :].rearrange("p c e -> p (c e)"), SC[:, 0, 0:KC * E]).then_inc(s["rawE"], 1)
            for n in range(2):
                dve.tensor_copy(sT[n][:, :, :].rearrange("p c i -> p (c i)"), SC[:, 1 + n, 0:KC * SI]).then_inc(s["rawE"], 1)
            dve.tensor_copy(sdT[:, :, :].rearrange("p m h -> p (m h)"), SC[0:I, 3, :]).then_inc(s["rawE"], 1)
            dve.wait_ge(s["pre"], 5)

            def gated(m, par):
                dve.wait_ge(s["sq"], m + 1)
                dve.tensor_reduce(ms[:, :], sq[:, :].rearrange("p (h d) -> p h d", d=D), AX.X, ALU.add).then_inc(s["ms"], 1)
                dve.wait_ge(s["eg"], m + 1)
                dve.reciprocal(sigm[:, :], eg1[:, :]).then_inc(s["sigm"], 1)
                dve.wait_ge(s["sigm"], m + 1)
                dve.tensor_tensor(sgate[:, :], OG[:, HID:2 * HID], sigm[:, :], ALU.mult).then_inc(s["sgt"], 1)
                dve.wait_ge(s["rs"], m + 1)
                dve.tensor_tensor(on[:, :].rearrange("p (h d) -> p h d", d=D),
                                  OG[:, 0:HID].rearrange("p (h d) -> p h d", d=D),
                                  rs[:, :].unsqueeze(2).to_broadcast([P, H, D]), ALU.mult).then_inc(s["on"], 1)
                dve.wait_ge(s["on"], m + 1)
                dve.wait_ge(s["sgt"], m + 1)
                dve.tensor_tensor(of[:, :], on[:, :], sgate[:, :], ALU.mult).then_inc(s["of"], 1)

            def causal(m, par):
                dve.wait_ge(s["sc"], m + 1)
                dve.nop(nofuse=True)
                dve.copy_predicated(Am[:, :, :, :], caus.unsqueeze(1).unsqueeze(1).to_broadcast([P, 4, 4, C]),
                                    SC[:, :, 0:256].rearrange("p j (u t) -> p j u t", t=C)).then_inc(s["am"], 1)

            def post_norm(m, par):
                if first(m):
                    dve.wait_ge(s["xall"], 16)
                dve.wait_ge(s["Wop"], m + 1)
                dve.tensor_tensor(y[:, :], x_all[:, bass.ds(m, 1), :].rearrange("p a h -> p (a h)"), tA[:, 0:HID],
                                  ALU.add).then_inc(s["y"], 1)
                dve.wait_ge(s["y"], m + 1)
                dve.bn_stats(bn6[:, :], y[:, :]).then_inc(s["bn"], 1)
                dve.wait_ge(s["bn"], m + 1)
                dve.nop(nofuse=True)
                dve.bn_aggr(mv[:, :], bn6[:, :]).then_inc(s["mv"], 1)
                dve.wait_ge(s["rst"], m + 1)
                if alive(m - 2, NT):
                    dve.wait_ge(d_scat[par], half(m - 2, par, K * 16))
                    dve.wait_ge(s["x1c"], m - 1)
                dve.tensor_scalar(x1r[par][:, 0:HID], y[:, :], mv[:, 0:1], rstd[:, :], ALU.subtract, ALU.mult)\
                    .then_inc(s["x1"], 1)

            def states(m, par):
                slot = m + m // TPB
                s_in = Sst[:, bass.ds(slot, 1), :].rearrange("p a (g n) -> p (a g) n", g=KC)
                s_out = Sst[:, bass.ds(slot + 1, 1), :].rearrange("p a (g n) -> p (a g) n", g=KC)
                dve.wait_ge(s["ab"], m + 1)
                if alive(m - 1, NT):
                    dve.wait_ge(s["S"], 2 * m)
                    dve.wait_ge(s["og"], m)
                for c, src, dst in ((0, s_in, Smid[:, :, :]), (1, Smid[:, :, :], s_out)):
                    if c:
                        dve.wait_ge(s["S"], 2 * m + 1)
                    for g in range(KC):
                        last = dve.scalar_tensor_tensor(Tst[c][:, g, :], src[:, g, :], fa[:, 2 * g + c:2 * g + c + 1], blk,
                                                        ALU.mult, ALU.mult)
                    last.then_inc(s[f"T{c}"], 1)
                    dve.wait_ge(s[f"T{c}"], m + 1)
                    dve.wait_ge(s[f"Pp{c}"], m + 1)
                    dve.tensor_tensor(Ust[:, :, :].rearrange("p g n -> p (g n)"), SC[:, c, 0:256],
                                      Tst[c][:, :, :].rearrange("p g n -> p (g n)"), ALU.add).then_inc(s["U"], 1)
                    dve.wait_ge(s["U"], 2 * m + c + 1)
                    dve.tensor_tensor(dst, Ust[:, :, :],
                                      fb[:, :].rearrange("p (g c) -> p g c", c=2)[:, :, c:c + 1].to_broadcast([P, KC, P]),
                                      ALU.mult).then_inc(s["S"], 1)

            def decay(m, par):
                dve.wait_ge(s["lnd"], m + 1)
                dve.scalar_tensor_tensor(gk[:, :, :].rearrange("p u s -> p (u s)"), tB[:, 256:512], 0.0, z_ln[:, :],
                                         ALU.min, ALU.subtract).then_inc(s["gk"], 1)
                dve.wait_ge(s["gk"], m + 1)
                dve.tensor_tensor_scan(Dc[:, :, :].rearrange("p u s -> p (u s)"),
                                       gk[:, :, :].rearrange("p u s -> p (u s)"), scan_keep, 0.0,
                                       ALU.add, ALU.mult).then_inc(s["Dc"], 1)

            def decayed(m, par):
                dve.wait_ge(s["qk"], m + 1)
                dve.wait_ge(s["ex"], m + 1)
                dve.tensor_tensor(Kh[:, :, :].rearrange("p g t -> p (g t)"), QK[:, HID:2 * HID], EK[:, :], ALU.mult)\
                    .then_inc(s["kh"], 1)
                dve.scalar_tensor_tensor(Qh[par][:, :, :].rearrange("p g t -> p (g t)"), QK[:, 0:HID], D ** -0.5,
                                         EQ[:, :], ALU.mult, ALU.mult).then_inc(s["qh"], 1)
                dve.wait_ge(s["kh"], m + 1)
                for h in range(2):
                    last = dve.tensor_scalar(Kbd[:, :, h, :], Kh[:, :, :].rearrange("p g (c t) -> p (g c) t", c=2),
                                             cst[:, C_PAR + h:C_PAR + h + 1], None, ALU.mult)
                last.then_inc(s["kbd"], 1)

            def route(m, par):
                dve.wait_ge(s["lgp"], m + 1)
                dve.tensor_copy(lg[:, :], tB[:, 0:E]).then_inc(s["lg"], 1)
                dve.wait_ge(s["lg"], m + 1)
                dve.nop(nofuse=True)
                dve.max(mx8[:, :], lg[:, :]).then_inc(s["mx"], 1)
                dve.wait_ge(s["mx"], m + 1)
                dve.tensor_scalar(nmx[:, :], mx8[:, 0:1], -1.0, None, ALU.mult).then_inc(s["nmx"], 1)
                dve.max_index(ix8[:, :], mx8[:, :], lg[:, :]).then_inc(s["ix"], 1)
                dve.wait_ge(s["ix"], m + 1)
                dve.tensor_copy(x1r[par][:, ICOL:ICOL + K], ix8[:, 0:K]).then_inc(s["idx"], 1)
                dve.tensor_copy(x1r[par][:, DCOL:DCOL + K], cst[:, bass.ds(C_D + m * K, K)]).then_inc(s["dtab"], 1)
                dve.wait_ge(s["idx"], m + 1)
                dve.tensor_tensor(oh[:, :, :], eiota.unsqueeze(1).to_broadcast([P, K, E]),
                                  x1r[par][:, ICOL:ICOL + K].unsqueeze(2).to_broadcast([P, K, E]), ALU.is_equal)\
                    .then_inc(s["oh"], 1)
                dve.wait_ge(s["oh"], m + 1)
                dve.tensor_reduce(sel[:, :], oh[:, :, :].rearrange("p k e -> p e k"), AX.X, ALU.add).then_inc(s["sel"], 1)
                dve.wait_ge(s["es"], m + 1)
                dve.reciprocal(erec[:, :], esum[:, :]).then_inc(s["rec"], 1)
                dve.wait_ge(s["rec"], m + 1)
                dve.tensor_scalar(x1r[par][:, WCOL:WCOL + K], e8[:, 0:K], erec[:, :], None, ALU.mult).then_inc(s["wr"], 1)

            def place(m, par):
                dve.wait_ge(s["cum"], m + 1)
                dve.tensor_tensor(sel_acc[:, :], sel_acc[:, :], sel[:, :], ALU.add).then_inc(s["acc"], 1)
                dve.tensor_tensor(pm[:, :, :], SC[:, 2, 0:E].unsqueeze(1).to_broadcast([P, K, E]), oh[:, :, :], ALU.mult)\
                    .then_inc(s["pm"], 1)
                dve.wait_ge(s["pm"], m + 1)
                dve.tensor_reduce(pos[:, :], pm[:, :, :], AX.X, ALU.add).then_inc(s["pos"], 1)
                dve.wait_ge(s["pos"], m + 1)
                dve.tensor_scalar(over[:, :], pos[:, :], CAP - 0.5, float(NOWHERE), ALU.is_ge, ALU.mult)
                dve.scalar_tensor_tensor(slot_f[:, :], x1r[par][:, ICOL:ICOL + K], float(CAP), pos[:, :], ALU.mult, ALU.add)\
                    .then_inc(s["sf"], 1)
                dve.wait_ge(s["sf"], m + 1)
                if alive(m - 2, NT):
                    dve.wait_ge(d_scat[par], half(m - 2, par, K * 16))
                dve.tensor_tensor(slot_u[par][:, :], slot_f[:, :], over[:, :], ALU.add).then_inc(s["slot"], 1)

            def tile_step(i, par):
                if alive(i - 1, NT):
                    gated(i - 1, 1 - par)
                if alive(i, NT):
                    causal(i, par)
                if alive(i - 1, NT):
                    post_norm(i - 1, 1 - par)
                if alive(i, NT):
                    states(i, par)
                if alive(i + 1, NT):
                    decay(i + 1, 1 - par)
                    decayed(i + 1, 1 - par)
                if alive(i - 2, NT):
                    place(i - 2, par)
                if alive(i - 1, NT):
                    route(i - 1, 1 - par)
            run_tiles(dve, tile_step)

            def shared(m):
                dve.wait_ge(s["sil"], m + 1)
                if not first(m):
                    dve.wait_ge(s["sdp"], m)
                u = SC[0:I, 2, :].rearrange("p (a n t) -> p a n t", a=SM, n=2)
                dve.tensor_tensor(sh_h[:, :, :], sh_g[:, :, :], u[:, :, 1, :], ALU.mult).then_inc(s["shh"], 1)
                dve.wait_ge(s["sdp"], m + 1)
                if first(m):
                    dve.wait_ge(s["x1c"], NT)
                dve.tensor_tensor(base[:, bass.ds(m, 1), :].rearrange("p a h -> p (a h)"),
                                  x1_all[:, bass.ds(m, 1), :].rearrange("p a h -> p (a h)"), SC[:, 3, 0:HID], ALU.add)\
                    .then_inc(s["base"], 1)
            shared(0)
            with dve.Fori(1, NT // 2) as m:
                shared(m)

            def pair_step(p, k):
                if alive(p, NP):
                    r = k % GXR
                    dve.wait_ge(d_gx[r], slot_count(p, k))
                    if alive(p - GXR, NP):
                        dve.wait_ge(s["ev"], p - GXR + 1)
                        dve.wait_ge(d_put[r], slot_count(p - GXR, r))
                    ecol = cst[:, bass.ds(C_ECOL + p, 1)]
                    dve.scalar_tensor_tensor(junk[:, :], gx[:, r, ICOL:ICOL + K], ecol, gx[:, r, WCOL:WCOL + K],
                                             ALU.is_equal, ALU.mult, accum_out=wsel[:, r:r + 1]).then_inc(s["wd"], 1)
                    dve.wait_ge(s["wd"], p + 1)
                    dve.scalar_tensor_tensor(junk[:, :], gx[:, r, ICOL:ICOL + K], ecol, gx[:, r, DCOL:DCOL + K],
                                             ALU.is_equal, ALU.mult, accum_out=dsel[:, r:r + 1]).then_inc(s["dsel"], 1)
                    dve.wait_ge(s["dsel"], p + 1)
                    dve.tensor_scalar(dest[r][:, :], dsel[:, r:r + 1], float(NOWHERE), None, ALU.add).then_inc(s["dest"], 1)
                if alive(p - 1, NP):
                    q = (k - 1) % 2
                    dve.wait_ge(s["sig"], p)
                    if alive(p - 3, NP):
                        dve.wait_ge(s["dn"], p - 2)
                    dve.tensor_tensor(hid[:, q, :], sg[:, q, :], GUb[q][0:I, P:2 * P], ALU.mult).then_inc(s["hid"], 1)
            run_pairs(dve, pair_step)
            with dve.Fori(NT // 2, NT) as m:
                shared(m)

            def finish(m, par):
                dve.wait_ge(d_cin[par], half(m, par, 16))
                dve.tensor_reduce(csum[:, :], cin[par][:, :].rearrange("p (k h) -> p h k", k=K), AX.X, ALU.add)\
                    .then_inc(s["csum"], 1)
                dve.wait_ge(s["csum"], m + 1)
                dve.tensor_tensor(yf[:, :], csum[:, :], base[:, bass.ds(m, 1), :].rearrange("p a h -> p (a h)"), ALU.add)\
                    .then_inc(s["yf"], 1)
                dve.wait_ge(s["yf"], m + 1)
                dve.bn_stats(bnf[:, :], yf[:, :]).then_inc(s["bnf"], 1)
                dve.wait_ge(s["bnf"], m + 1)
                dve.nop(nofuse=True)
                dve.nop(nofuse=True)
                dve.bn_aggr(mvf[:, :], bnf[:, :]).then_inc(s["mvf"], 1)
                dve.wait_ge(s["rsf"], m + 1)
                if not (isinstance(m, int) and m < 2):
                    dve.wait_ge(d_out[par], half(m - 2, par, 16))
                dve.tensor_scalar(res[par][:, :], yf[:, :], mvf[:, 0:1], rstdf[:, :], ALU.subtract, ALU.mult)\
                    .then_inc(s["res"], 1)
            dve.wait_ge(s["base"], NT)
            finish(0, 0)
            finish(1, 1)
            with dve.Fori(1, NT // 2) as h:
                finish(h * 2, 0)
                finish(h * 2 + 1, 1)


_INS = ["L0_attn_x", "L0_attn_Wq", "L0_attn_Wk", "L0_attn_Wv", "L0_attn_Wg1", "L0_attn_Wg2", "L0_attn_bg2",
        "L0_attn_Wgate", "L0_attn_norm_w", "L0_attn_Wo", "L0_ffn_gate_w", "L0_ffn_gate_up_proj", "L0_ffn_down_proj",
        "L0_ffn_shared_gate_w", "L0_ffn_shared_up_w", "L0_ffn_shared_down_w"]


def kernel(**inputs):
    import concourse.bacc as bacc
    from concourse.bass_utils import run_bass_kernel_spmd

    nc = bacc.Bacc("TRN2", target_bir_lowering=False, num_devices=1)
    arrays = {"consts": constants()}
    args = [nc.dram_tensor("consts", arrays["consts"].shape, F32, kind="ExternalInput").ap()]
    for name in _INS:
        a = np.ascontiguousarray(inputs[name])
        arrays[f"in_{name}"] = a
        args.append(nc.dram_tensor(f"in_{name}", a.shape, mybir.dt.from_np(a.dtype), kind="ExternalInput").ap())
    args.append(nc.dram_tensor("result", (B, L, HID), F32, kind="ExternalOutput").ap())
    build(nc, *args)
    r = run_bass_kernel_spmd(nc, [arrays], core_ids=[0])
    return r.results[0]["result"]
```

```python
from contextlib import ExitStack

import numpy as np

import concourse.bass as bass
import concourse.mybir as mybir

F32 = mybir.dt.float32
U32 = mybir.dt.uint32
I32 = mybir.dt.int32
ALU = mybir.AluOpType
ACT = mybir.ActivationFunctionType
AX = mybir.AxisListType

P = 128
B, L, HID = 2, 512, 256
T = B * L
NT = T // P
TPB = L // P
KC = HID // P
H, D = 16, 16
C = 64
LOWR = 16
GLN = 16.0
EPS = 1e-5
E, K, CAP = 64, 6, 64
I = 96
SI = 192
SM = SI // I
NP = E // 2
ROW = HID + 3 * K
WCOL, ICOL, DCOL = HID, HID + K, HID + 2 * K
NOWHERE = 8192
RING = 14
GXR = 7
HEAD, TAIL = 4, 2

C_ID, C_BLK, C_TRI, C_ONE, C_CAUS, C_SCAN, C_EI, C_D, C_ECOL, C_PAR, C_EPS, C_END = np.cumsum(
    [0, P, P, P, P, C, KC * P, E, NT * K, NP, 2, 1]).tolist()


def constants():
    c = np.zeros((P, C_END), np.float32)
    p = np.arange(P)
    c[:, C_ID:C_ID + P] = np.eye(P)
    c[:, C_BLK:C_BLK + P] = p[:, None] // D == p[None, :] // D
    c[:, C_TRI:C_TRI + P] = p[:, None] < p[None, :]
    c[:, C_ONE:C_ONE + P] = 1.0
    c[:, C_CAUS:C_CAUS + C] = p[:, None] % C <= np.arange(C)[None, :]
    c[:, C_SCAN:C_SCAN + KC * P] = np.arange(KC * P) % C != 0
    c[:, C_EI:C_EI + E] = np.arange(E)
    token = np.arange(NT)[None, :, None] * P + p[:, None, None]
    c[:, C_D:C_D + NT * K] = (token * K + np.arange(K)[None, None, :] - NOWHERE).reshape(P, NT * K)
    c[:, C_ECOL:C_ECOL + NP] = 2 * np.arange(NP)[None, :] + p[:, None] // C
    c[:, C_PAR:C_PAR + 2] = (p[:, None] // D) % 2 == np.arange(2)[None, :]
    c[:, C_EPS] = EPS
    return c


def alive(m, n):
    return not isinstance(m, int) or 0 <= m < n


def first(m):
    return isinstance(m, int) and m == 0


def build(nc, consts, x, Wq, Wk, Wv, Wg1, Wg2, bg2, Wgate, norm_w, Wo, gate_w, gup, down, sg_w, su_w, sd_w, out):
    slots = nc.dram_tensor("slot_rows", [E * CAP, ROW], F32, kind="Internal").ap()
    parts = nc.dram_tensor("choice_rows", [T * K, HID], F32, kind="Internal").ap()
    x_rows = x.rearrange("b (t p) h -> (b t) p h", p=P)
    out_rows = out.rearrange("b (t p) h -> (b t) p h", p=P)

    with ExitStack() as ctx:
        def sb(name, shape, dt=F32):
            return ctx.enter_context(nc.sbuf_tensor(name, shape, dt))

        def ps(name, shape):
            return ctx.enter_context(nc.psum_tensor(name, shape, F32))

        def sem(name):
            return ctx.enter_context(nc.semaphore(name))

        cst = sb("cst", [P, C_END])
        ident, blk, tri, ones = (cst[:, a:a + P] for a in (C_ID, C_BLK, C_TRI, C_ONE))
        caus = cst[:, C_CAUS:C_CAUS + C].bitcast(I32)
        scan_keep = cst[:, C_SCAN:C_SCAN + KC * P]
        eiota = cst[:, C_EI:C_EI + E]
        eps_col = cst[:, C_EPS:C_EPS + 1]
        wq, wk, wv, wg, wo = (sb(n, [P, KC, HID]) for n in ("wq", "wk", "wv", "wg", "wo"))
        wg1 = sb("wg1", [P, KC, LOWR])
        wg2 = sb("wg2", [LOWR + 1, HID])
        nw_col = sb("nw_col", [P, 1])
        raw_g = sb("raw_g", [E, HID])
        raw_s = [sb(n, [I, SM, HID]) for n in ("raw_sg", "raw_su")]
        raw_d = sb("raw_d", [P, KC, SI])
        gwT = sb("gwT", [P, KC, E])
        sT = [sb(n, [P, KC, SI]) for n in ("sgT", "suT")]
        sdT = sb("sdT", [I, SM, HID])
        late = sb("late", [P, NT * HID])
        x_all = late[:, 0:NT * HID].rearrange("p (t h) -> p t h", t=NT)
        gx = late[:, 0:GXR * ROW].rearrange("p (g n) -> p g n", g=GXR)
        x_in = [sb(f"x_in{b}", [P, HID]) for b in range(2)]
        xT = sb("xT", [P, KC, P])
        xTd = sb("xTd", [P, KC * 2, 2, C])
        low = sb("low", [LOWR + 1, P])
        Vbd = [sb(f"Vbd{b}", [P, 16, 2 * D]) for b in range(2)]
        Vz = [sb(f"Vz{b}", [P, 2, HID]) for b in range(2)]
        soft = sb("soft", [P, 4, 2 * HID])
        z_abs, z_exp, z_ln, lsg = (soft[:, n, :] for n in range(4))
        gk = lsg[:, 0:HID].rearrange("p (u s) -> p u s", s=C)
        sigm = sb("sigm", [P, HID])
        Qbd = sb("Qbd", [P, KC * 2, 4, C])
        Dc = sb("Dc", [P, KC * 2, C])
        EQ = sb("EQ", [P, KC * P])
        EK = sb("EK", [P, KC * P])
        fa = [sb(f"fa{b}", [P, KC * 2]) for b in range(2)]
        fb = [sb(f"fb{b}", [P, KC * 2]) for b in range(2)]
        Qh = [sb(f"Qh{b}", [P, KC, P]) for b in range(2)]
        Kh = sb("Kh", [P, KC, P])
        Kbd = sb("Kbd", [P, KC * 2, 2, C])
        Kt = sb("Kt", [P, HID])
        Am = sb("Am", [P, 4, 4, C])
        Tst = [sb(f"Tst{c}", [P, KC, P]) for c in range(2)]
        Umid = sb("Umid", [P, KC, P])
        fc = sb("fc", [P, 2, KC])
        Sst = sb("Sst", [P, NT + B, KC * P])
        sq = sb("sq", [P, HID])
        ms = sb("ms", [P, H])
        ms_ln = sb("ms_ln", [P, H])
        rs = sb("rs", [P, H])
        sgate = [sb(f"sgate{b}", [P, HID]) for b in range(2)]
        on = sb("on", [P, HID])
        of = sb("of", [P, HID])
        oT = sb("oT", [P, KC, P])
        y = sb("y", [P, HID])
        bn6 = sb("bn6", [P, 6])
        mv = sb("mv", [P, 2])
        v_ln = sb("v_ln", [P, 1])
        rstd = sb("rstd", [P, 1])
        x1s = [sb(f"x1s{b}", [P, HID]) for b in range(2)]
        x1T = sb("x1T", [P, KC, P])
        x1_all = sb("x1_all", [P, NT, HID])
        rows = [sb(f"rows{b}", [P, ROW]) for b in range(2)]
        idx_f = sb("idx_f", [P, K])
        x1T_all = sb("x1T_all", [P, NT, KC * P])
        lg = sb("lg", [P, E])
        mx8 = sb("mx8", [P, 8])
        ix8 = sb("ix8", [P, 8], U32)
        nmx = sb("nmx", [P, 1])
        e64 = sb("e64", [P, E])
        e8 = sb("e8", [P, 8])
        esum = sb("esum", [P, 1])
        erec = sb("erec", [P, 1])
        oh = sb("oh", [P, K, E])
        sel = sb("sel", [P, E])
        sel_acc = sb("sel_acc", [P, E])
        pm = sb("pm", [P, K, E])
        pos = sb("pos", [P, K])
        over = sb("over", [P, K])
        slot_f = sb("slot_f", [P, K])
        slot_u = [sb(f"slot_u{b}", [P, K], U32) for b in range(2)]
        filler = sb("filler", [P, 2, ROW])
        zeros = sb("zeros", [P, 3 * HID])
        wgu_r = sb("wgu_r", [P, RING, 2 * KC, 2 * I])
        wdn_r = sb("wdn_r", [I, RING, 2, HID])
        gxT = Sst[:, 0:2, :]
        sg = Sst[0:I, 2, :].rearrange("p (a t) -> p a t", a=2)
        hid = Sst[0:I, 3, :].rearrange("p (a t) -> p a t", a=2)
        junk = sb("junk", [P, K])
        wsel = sb("wsel", [P, GXR])
        dsel = sb("dsel", [P, GXR])
        dest = [sb(f"dest{b}", [P, 1], U32) for b in range(GXR)]
        eo = [soft[:, b // 2, b % 2 * HID:(b % 2 + 1) * HID] for b in range(GXR)]
        sh_g = [sb(f"sh_g{b}", [I, SM, P]) for b in range(2)]
        sh_h = [sb(f"sh_h{b}", [I, SM, P]) for b in range(2)]
        base = x1_all
        cin = [wgu_r[:, 2 * m:2 * m + 2, :, :].rearrange("p a b n -> p (a b n)") for m in range(RING // 2)]
        cin += [late[:, 0:K * HID]] * (NT - RING // 2)
        half_sum = [x1T_all[:, b * K // 2:(b + 1) * K // 2, :].rearrange("p a n -> p (a n)") for b in range(2)]
        bnf = sb("bnf", [P, 6])
        mvf = sb("mvf", [P, 2])
        vf_ln = sb("vf_ln", [P, 1])
        rstdf = sb("rstdf", [P, 1])
        res = [Sst[:, 6 + b, :] for b in range(2)]

        tA, tB, QK, VO, PX, X7 = (ps(n, [P, 512]) for n in ("tA", "tB", "QK", "VO", "PX", "X7"))
        SC = ps("SC", [P, 4, 4 * C])
        SCb = SC[:, :, :].rearrange("p (b u) n -> p b (u n)", b=2)
        OG = VO
        XTb, GUb, DNb = (tA, tB), (QK, VO), (PX, X7)

        SHb = (QK, tB)
        SDb = CSb = (SC[:, 0, :], SC[:, 2, :])

        s = {}
        for n in ("cst w_low w_val w_gate w_qk raw nw xall fill zero pre prefilled wo_ready low1 "
                  "rawT rawE xTp xT lowp low Vp V zp qk absd expd lnd gk Dc ex ab kh qh kbd khTp Kt sc am fc Pp T0 T1 U "
                  "og sq sigm qbd ms msl rs sgt on of oTp oT Wop y bn mv vl rst x1 x1Tp x1T x1c x1Tc lgp lg mx ix nmx es idx oh "
                  "sel wr cum acc pm pos sf slot xrow rec "
                  "xtp xt gu sig hid dn ev wd dsel dest "
                  "sgp sil shh sdp base hsum csp bnf mvf vfl rsf res").split():
            s[n] = sem("s_" + n)
        d_xin = [sem(f"d_xin{b}") for b in range(2)]
        d_scat = [sem(f"d_scat{b}") for b in range(2)]
        d_w = [sem(f"d_w{k}") for k in range(RING)]
        d_gx = [sem(f"d_gx{k}") for k in range(GXR)]
        d_put = [sem(f"d_put{k}") for k in range(GXR)]
        d_cin = [sem(f"d_cin{m}") for m in range(NT)]
        d_out = [sem(f"d_out{b}") for b in range(2)]
        NRAW = 5 * 16

        def half(m, par, per):
            return (m + (1 if par else 2)) * (per // 2)

        def run_tiles(eng, body):
            for i in range(-2, 2):
                body(i, i % 2)
            with eng.Fori(1, NT // 2 - 1) as h:
                body(h * 2, 0)
                body(h * 2 + 1, 1)
            for i in range(NT - 2, NT + 2):
                body(i, i % 2)

        def run_pairs(eng, body):
            for k in range(HEAD):
                body(k, k, 0)
            with eng.Fori(0, (NP + 2 - HEAD - TAIL) // RING) as h:
                for k in range(HEAD, HEAD + RING):
                    body(h * RING + k, k, h)
            for p in range(NP + 2 - TAIL, NP + 2):
                body(p, p, 0)

        def run_shared(eng, body):
            with eng.Fori(2, NT // 2) as h:
                body(h * 2, 0)
                body(h * 2 + 1, 1)
            body(NT, 0)

        def slot_loads(k, h):
            return h * (16 * RING // GXR) + (k // GXR + 1) * 16

        def put_done(k, h):
            return h * (16 * RING // GXR) + (k // GXR + 2) * 16

        def weight_loads(k, h):
            return h * 32 + (k // RING + 1) * 32

        block = ctx.enter_context(nc.Block())

        @block.sync
        def _(sp):
            def load_x(m, par):
                sp.dma_start(x_in[par][:, :], x_rows[m]).then_inc(d_xin[par], 16)

            sp.dma_start(cst[:, :], consts).then_inc(s["cst"], 16)
            load_x(0, 0)
            load_x(1, 1)
            def load_weight(t, w, n):
                sp.dma_start(t[:, :, :], w.rearrange("(c p) n -> p c n", p=P)).then_inc(s[n], 16)
            load_weight(wg1, Wg1, "w_low")
            load_weight(wv, Wv, "w_val")
            load_weight(wg, Wgate, "w_gate")
            sp.dma_start(wg2[0:LOWR, :], Wg2).then_inc(s["w_gate"], 16)
            sp.dma_start(wg2[LOWR:LOWR + 1, :], bg2.rearrange("(a n) -> a n", a=1)).then_inc(s["w_gate"], 16)
            load_weight(wq, Wq, "w_qk")
            load_weight(wk, Wk, "w_qk")
            sp.dma_start(x_all[:, :, :], x_rows.rearrange("t p h -> p t h")).then_inc(s["xall"], 16)
            for h in range(P // D):
                sp.dma_start(nw_col[h * D:(h + 1) * D, :], norm_w.rearrange("(d a) -> d a", a=1)).then_inc(s["nw"], 16)

            sp.wait_ge(s["fill"], 2)
            sp.dma_start(slots.rearrange("(p a) n -> p a n", p=P),
                          filler[:, 0:1, :].to_broadcast([P, E * CAP // P, ROW])).then_inc(s["prefilled"], 16)

            def load_weights(q, k):
                sp.dma_start(wgu_r[:, k, :, :], gup[bass.ds(q * 2, 2)].rearrange("e (c p) n -> p (e c) n", p=P))\
                    .then_inc(d_w[k], 16)
                sp.dma_start(wdn_r[:, k, :, :], down[bass.ds(q * 2, 2)].rearrange("e p n -> p e n")).then_inc(d_w[k], 16)

            def load_slots(p):
                sp.dma_start(gx[:, p % GXR, :], slots[p * P:(p + 1) * P]).then_inc(d_gx[p % GXR], 16)

            for m in range(2, NT):
                sp.wait_ge(s["xTp"], m - 1)
                load_x(m, m % 2)
                for q in range(2 * m - 4, 2 * m - 2):
                    load_weights(q, q)
            sp.wait_ge(s["xTp"], NT)
            for q in range(2 * NT - 4, RING):
                load_weights(q, q)
            for par in range(2):
                sp.wait_ge(d_scat[par], half(NT - 2 + par, par, K * 16))
            for p in range(GXR):
                load_slots(p)
            for p in range(GXR, NP):
                sp.wait_ge(s["xtp"], p - GXR + 1)
                sp.wait_ge(s["dsel"], p - GXR + 1)
                load_slots(p)
                q = p + RING - GXR
                if q < NP:
                    sp.wait_ge(s["dn"], q - RING + 1)
                    load_weights(q, q % RING)

            for k in range(GXR):
                sp.wait_ge(d_put[k], 16 * (1 + len(range(k, NP, GXR))))
            for m in range(NT):
                sp.dma_start(cin[m], parts[m * P * K:(m + 1) * P * K].rearrange("(p k) h -> p (k h)", k=K))\
                    .then_inc(d_cin[m], 16)

            def store(m, par):
                sp.wait_ge(s["res"], m + 1)
                sp.dma_start(out_rows[bass.ds(m, 1)].rearrange("a p h -> (a p) h"), res[par][:, :]).then_inc(d_out[par], 16)
            with sp.Fori(0, NT // 2) as h:
                for par in range(2):
                    store(h * 2 + par, par)
            for par in range(2):
                sp.wait_ge(d_out[par], 16 * (NT // 2))

        @block.gpsimd
        def _(pool):
            pool.memset(filler[:, :, :], 0.0).then_inc(s["fill"], 1)
            pool.wait_ge(s["fill"], 1)
            pool.memset(filler[:, :, ICOL:ICOL + K], -1.0).then_inc(s["fill"], 1)
            pool.memset(zeros[:, :], 0.0).then_inc(s["zero"], 1)
            for b in range(2):
                pool.memset(Vbd[b][:, :, :], 0.0).then_inc(s["pre"], 1)
                pool.memset(Vz[b][:, :, :], 0.0).then_inc(s["pre"], 1)
            pool.memset(Qbd[:, :, :, :], 0.0).then_inc(s["pre"], 1)
            pool.memset(Am[:, :, :, :], 0.0).then_inc(s["pre"], 1)
            pool.memset(fb[1][:, :], 1.0).then_inc(s["pre"], 1)
            pool.memset(sel_acc[:, :], 0.0).then_inc(s["pre"], 1)
            pool.memset(low[:, :], 1.0).then_inc(s["low1"], 1)
            for b in range(B):
                pool.memset(Sst[:, b * (TPB + 1), :], 0.0).then_inc(s["pre"], 1)
            pool.wait_ge(s["zero"], 1)
            for k in range(GXR):
                a, b = k * T // P // GXR, (k + 1) * T // P // GXR
                pool.dma_start(parts.rearrange("(p a) n -> p a n", p=P)[:, a * K:b * K, :].rearrange("p (a b) n -> p a (b n)", b=3),
                               zeros[:, :].unsqueeze(1).to_broadcast([P, (b - a) * K // 3, 3 * HID])).then_inc(d_put[k], 16)

            def keep(m, par):
                pool.wait_ge(s["x1"], m + 1)
                pool.tensor_copy(x1_all[:, bass.ds(m, 1), :].rearrange("p a h -> p (a h)"), x1s[par][:, :])\
                    .then_inc(s["x1c"], 1)
                pool.wait_ge(s["x1T"], m + 1)
                pool.tensor_copy(x1T_all[:, bass.ds(m, 1), :].rearrange("p a h -> p (a h)"),
                                 x1T[:, :, :].rearrange("p c t -> p (c t)")).then_inc(s["x1Tc"], 1)

            def dispatch(m, par):
                if alive(m - 2, NT):
                    pool.wait_ge(d_scat[par], half(m - 2, par, K * 16))
                pool.wait_ge(s["x1c"], m + 1)
                pool.nop(nofuse=True)
                pool.tensor_copy(rows[par][:, 0:HID], x1_all[:, bass.ds(m, 1), :].rearrange("p a h -> p (a h)"))\
                    .then_inc(s["xrow"], 1)
                pool.wait_ge(s["xrow"], m + 1)
                pool.wait_ge(s["slot"], m + 1)
                pool.wait_ge(s["wr"], m + 1)
                pool.nop(nofuse=True)
                for k in range(K):
                    pool.indirect_dma_start(slots, bass.IndirectOffsetOnAxis(ap=slot_u[par][:, k:k + 1], axis=0),
                                            rows[par][:, :], None, bounds_check=last_slot,
                                            oob_is_err=False).then_inc(d_scat[par], 16)

            def tile_step(i, par):
                if alive(i - 1, NT):
                    keep(i - 1, 1 - par)
                if alive(i - 2, NT):
                    dispatch(i - 2, par)
            last_slot, last_part = pool.to_reg(E * CAP - 1), pool.to_reg(T * K - 1)
            pool.wait_ge(s["prefilled"], 16)
            run_tiles(pool, tile_step)
            for k in range(GXR):
                pool.wait_ge(d_put[k], 16)

            def put(p, k, h):
                if k >= 2:
                    q = (k - 2) % GXR
                    pool.wait_ge(s["dest"], p - 1)
                    pool.wait_ge(s["ev"], p - 1)
                    pool.nop(nofuse=True)
                    pool.indirect_dma_start(parts, bass.IndirectOffsetOnAxis(ap=dest[q][:, :], axis=0),
                                            eo[q][:, :], None, bounds_check=last_part, oob_is_err=False)\
                        .then_inc(d_put[q], 16)
            run_pairs(pool, put)

        @block.tensor
        def _(pe):
            def mm(o, a, b, start, stop=True):
                return pe.matmul(o, a, b, start=start, stop=stop, skip_group_check=True)

            def t_weights():
                pe.wait_ge(s["raw"], NRAW)
                pe.wait_ge(s["V"], 1)
                pe.wait_ge(s["xT"], 2)
                for c in range(KC):
                    pe.transpose(tA[:, 256 + c * E:256 + (c + 1) * E], raw_g[:, c * P:(c + 1) * P], ident[0:E, 0:E])
                for n, bank in enumerate((VO, PX)):
                    for c in range(KC):
                        for m in range(SM):
                            pe.transpose(bank[:, c * SI + m * I:c * SI + (m + 1) * I],
                                         raw_s[n][:, m, c * P:(c + 1) * P], ident[0:I, 0:I])
                for m in range(SM):
                    for c in range(KC):
                        last = pe.transpose(X7[0:I, m * HID + c * P:m * HID + (c + 1) * P],
                                            raw_d[:, c, m * I:(m + 1) * I], ident)
                last.then_inc(s["rawT"], 1)

            def t_x(m, par):
                if first(m):
                    pe.wait_ge(s["cst"], 16)
                pe.wait_ge(d_xin[par], half(m, par, 16))
                if alive(m - 3, NT):
                    pe.wait_ge(s["y"], m - 2)
                for c in range(KC):
                    last = pe.transpose(tA[:, c * P:(c + 1) * P], x_in[par][:, c * P:(c + 1) * P], ident)
                last.then_inc(s["xTp"], 1)

            def t_k(m, par):
                pe.wait_ge(s["kh"], m + 1)
                pe.wait_ge(s["qh"], m + 1)
                for c in range(KC):
                    last = pe.transpose(QK[:, c * P:(c + 1) * P], Kh[:, c, :], ident)
                last.then_inc(s["khTp"], 1)

            def scores(m, par):
                pe.wait_ge(s["kbd"], m + 1)
                pe.wait_ge(s["qbd"], 2 * m + 2)
                if alive(m - 1, NT):
                    pe.wait_ge(s["am"], m)
                for u in range(KC * 2):
                    last = mm(SC[:, u, :], Kbd[:, u, :, :].rearrange("p a s -> p (a s)"),
                              Qbd[:, u, :, :].rearrange("p j s -> p (j s)"), True)
                last.then_inc(s["sc"], 1)

            def t_o(m, par):
                pe.wait_ge(s["of"], m + 1)
                if alive(m + 2, NT):
                    pe.wait_ge(s["xT"], m + 3)
                for c in range(KC):
                    last = pe.transpose(tA[:, 256 + c * P:256 + (c + 1) * P], of[:, c * P:(c + 1) * P], ident)
                last.then_inc(s["oTp"], 1)

            def low_rank(m, par):
                pe.wait_ge(s["xT"], m + 1)
                if first(m):
                    pe.wait_ge(s["w_low"], 16)
                if alive(m - 1, NT):
                    pe.wait_ge(s["Kt"], m)
                for c in range(KC):
                    last = mm(QK[0:LOWR, 0:P], wg1[:, c, :], xT[:, c, :], c == 0, c == KC - 1)
                last.then_inc(s["lowp"], 1)

            def values(m, par):
                if first(m):
                    pe.wait_ge(s["w_val"], 16)
                if alive(m - 2, NT):
                    pe.wait_ge(s["on"], m - 1)
                for a in range(2):
                    for c in range(KC):
                        last = mm(VO[:, a * HID:(a + 1) * HID], xTd[:, 2 * c + a, :, :].rearrange("p h t -> p (h t)"),
                                  wv[:, c, :], c == 0, c == KC - 1)
                last.then_inc(s["Vp"], 1)

            def gates(m, par):
                if alive(m - 1, NT):
                    pe.wait_ge(s["sgt"], m)
                if first(m):
                    pe.wait_ge(s["w_gate"], 3 * 16)
                for c in range(KC):
                    mm(tB[:, HID:2 * HID], xT[:, c, :], wg[:, c, :], c == 0, c == KC - 1)
                pe.wait_ge(s["low"], m + 1)
                for g in range(KC):
                    last = mm(tB[:, g * P:(g + 1) * P], wg2[:, g * P:(g + 1) * P], low[:, :], False)
                last.then_inc(s["zp"], 1)

            def queries_keys(m, par):
                if first(m):
                    pe.wait_ge(s["w_qk"], 2 * 16)
                for w, o in ((wq, 0), (wk, HID)):
                    for g in range(KC):
                        for c in range(KC):
                            last = mm(QK[:, o + g * P:o + (g + 1) * P], w[:, c, g * P:(g + 1) * P],
                                      xT[:, c, :], c == 0, c == KC - 1)
                last.then_inc(s["qk"], 1)

            def out_proj(m, par):
                pe.wait_ge(s["oT"], m + 1)
                if first(m):
                    pe.wait_ge(s["wo_ready"], 2)
                for c in range(KC):
                    last = mm(tA[:, 0:HID], oT[:, c, :], wo[:, c, :], c == 0, c == KC - 1)
                last.then_inc(s["Wop"], 1)

            def state(m, par):
                pe.wait_ge(s["Kt"], m + 1)
                pe.wait_ge(s["V"], m + 1)
                if first(m):
                    pe.wait_ge(s["rawE"], 4)
                if alive(m - 1, NT):
                    pe.wait_ge(s["U"], 2 * m)
                if alive(m - 3, NT):
                    pe.wait_ge(s["pm"], m - 2)
                for g in range(KC):
                    last = mm(PX[:, g * HID:(g + 1) * HID].rearrange("p (c n) -> p c n", c=2), Kt[:, g * P:(g + 1) * P],
                              Vz[par][:, :, g * P:(g + 1) * P], True)
                last.then_inc(s["Pp"], 1)

            def t_x1(m, par):
                pe.wait_ge(s["x1"], m + 1)
                for c in range(KC):
                    last = pe.transpose(X7[:, c * P:(c + 1) * P], x1s[par][:, c * P:(c + 1) * P], ident)
                last.then_inc(s["x1Tp"], 1)

            def count(m, par):
                pe.wait_ge(s["sel"], m + 1)
                if alive(m - 1, NT):
                    pe.wait_ge(s["acc"], m)
                    pe.wait_ge(s["pm"], m)
                if alive(m + 2, NT):
                    pe.wait_ge(s["U"], 2 * m + 6)
                mm(PX[:, 0:E], tri, sel[:, :], True, False)
                mm(PX[:, 0:E], ones, sel_acc[:, :], False).then_inc(s["cum"], 1)

            def attend(m, par):
                if alive(m + 1, NT):
                    pe.wait_ge(s["V"], m + 2)
                pe.wait_ge(s["am"], m + 1)
                for c in range(2):
                    for u in range(P // D):
                        g, j = u // 4, u % 4
                        mm(OG[c * C:(c + 1) * C, u * 32:(u + 1) * 32], Am[:, 2 * g + c, j, :],
                           Vbd[par][:, 8 * c + u, :], u == 0, False)

            def attend_state(m, par):
                for c in range(2):
                    pe.wait_ge(s[f"T{c}"], m + 1)
                    for g in range(KC):
                        last = mm(OG[c * C:(c + 1) * C, g * P:(g + 1) * P], Qh[par][:, g, c * C:(c + 1) * C],
                                  Tst[c][:, g, :], False)
                last.then_inc(s["og"], 1)

            def logits(m, par):
                pe.wait_ge(s["x1T"], m + 1)
                if alive(m - 1, NT):
                    pe.wait_ge(s["lg"], m)
                for c in range(KC):
                    last = mm(X7[:, HID:HID + E], x1T[:, c, :], gwT[:, c, :], c == 0, c == KC - 1)
                last.then_inc(s["lgp"], 1)

            def shared_step(m, par):
                if alive(m, NT):
                    pe.wait_ge(s["x1Tc"], m + 1)
                    if alive(m - 2, NT):
                        pe.wait_ge(s["shh"], m - 1)
                    elif par:
                        pe.wait_ge(s["sgt"], NT)
                    else:
                        pe.wait_ge(s["Kt"], NT)
                    xt = x1T_all[:, bass.ds(m, 1), :]
                    for a in range(SM):
                        for n in range(2):
                            for c in range(KC):
                                last = mm(SHb[par][0:I, (2 * a + n) * P:(2 * a + n + 1) * P], sT[n][:, c, a * I:(a + 1) * I],
                                          xt[:, :, c * P:(c + 1) * P].rearrange("p a t -> p (a t)"), c == 0, c == KC - 1)
                    last.then_inc(s["sgp"], 1)
                if alive(m - 1, NT):
                    pe.wait_ge(s["shh"], m)
                    if alive(m - 3, NT):
                        pe.wait_ge(s["base"], m - 2)
                    else:
                        pe.wait_ge(s["am"], NT)
                    for a in range(SM):
                        last = mm(SDb[1 - par], sh_h[1 - par][:, a, :], sdT[:, a, :], a == 0, a == SM - 1)
                    last.then_inc(s["sdp"], 1)

            def tile_step(i, par):
                now, nxt, prev = alive(i, NT), alive(i + 1, NT), alive(i - 1, NT)
                at_end = isinstance(i, int) and i >= NT
                if now:
                    state(i, par)
                if at_end:
                    shared_step(2 * (i - NT), 0)
                if nxt:
                    low_rank(i + 1, 1 - par)
                    values(i + 1, 1 - par)
                    gates(i + 1, 1 - par)
                if prev:
                    out_proj(i - 1, 1 - par)
                if nxt:
                    queries_keys(i + 1, 1 - par)
                if now:
                    attend(i, par)
                    attend_state(i, par)
                if at_end:
                    shared_step(2 * (i - NT) + 1, 1)
                if alive(i - 2, NT):
                    count(i - 2, par)
                if alive(i + 2, NT):
                    t_x(i + 2, par)
                if prev:
                    t_x1(i - 1, 1 - par)
                if nxt:
                    t_k(i + 1, 1 - par)
                    scores(i + 1, 1 - par)
                if now:
                    t_o(i, par)
                if prev:
                    logits(i - 1, 1 - par)
                if isinstance(i, int) and i == -1:
                    t_weights()
            run_tiles(pe, tile_step)
            run_shared(pe, shared_step)

            def pair_step(p, k, h):
                if alive(p, NP):
                    pe.wait_ge(d_gx[k % GXR], slot_loads(k, h))
                    if alive(p - 2, NP):
                        pe.wait_ge(s["xt"], p - 1)
                    elif p == 1:
                        pe.wait_ge(s["shh"], NT)
                    for c in range(KC):
                        last = pe.transpose(XTb[k % 2][:, c * P:(c + 1) * P], gx[:, k % GXR, c * P:(c + 1) * P], ident)
                    last.then_inc(s["xtp"], 1)
                if alive(p - 1, NP):
                    q, r = (k - 1) % 2, (k - 1) % RING
                    pe.wait_ge(d_w[r], weight_loads(k - 1, h))
                    pe.wait_ge(s["xt"], p)
                    if alive(p - 3, NP):
                        pe.wait_ge(s["hid"], p - 2)
                    for e in range(2):
                        for n in range(2):
                            for c in range(KC):
                                o = (2 * n + e) * CAP
                                last = mm(GUb[q][0:I, o:o + CAP], wgu_r[:, r, 2 * e + c, n * I:(n + 1) * I],
                                          gxT[:, q, c * P + e * CAP:c * P + (e + 1) * CAP], c == 0, c == KC - 1)
                    last.then_inc(s["gu"], 1)
                if alive(p - 2, NP):
                    q, r = k % 2, (k - 2) % RING
                    pe.wait_ge(s["hid"], p - 1)
                    if alive(p - 4, NP):
                        pe.wait_ge(s["ev"], p - 3)
                    elif p == 2:
                        pe.wait_ge(s["base"], NT)
                    for e in range(2):
                        last = mm(DNb[q][e * CAP:(e + 1) * CAP, 0:HID], hid[:, q, e * CAP:(e + 1) * CAP],
                                  wdn_r[:, r, e, :], True)
                    last.then_inc(s["dn"], 1)
            run_pairs(pe, pair_step)

            for m in range(NT):
                pe.wait_ge(s["hsum"], m + 1)
                if m >= 2:
                    pe.wait_ge(s["res"], m - 1)
                for k in range(K // 2):
                    mm(CSb[m % 2], ident, half_sum[m % 2][:, k * HID:(k + 1) * HID], k == 0, False)
                mm(CSb[m % 2], ident, base[:, m, :], False).then_inc(s["csp"], 1)

        @block.scalar
        def _(act):
            act.preload_act_table_set("natural_log_exp_and_others")

            def copy(o, i):
                return act.activation(o, i, ACT.Copy)

            def gate_in(m, par):
                act.wait_ge(s["og"], m + 1)
                act.activation(sq[:, :], OG[:, 0:HID], ACT.Square).then_inc(s["sq"], 1)

            def rms(m, par):
                act.wait_ge(s["ms"], m + 1)
                act.activation(ms_ln[:, :], ms[:, :], ACT.Ln, bias=eps_col, scale=1.0 / D).then_inc(s["msl"], 1)
                act.wait_ge(s["msl"], m + 1)
                act.activation(rs[:, :], ms_ln[:, :], ACT.Exp, scale=-0.5).then_inc(s["rs"], 1)

            def ev_x(m, par):
                act.wait_ge(s["xTp"], m + 1)
                copy(xT[:, :, :].rearrange("p c t -> p (c t)"), tA[:, 0:256])
                copy(xTd[:, :, :, :], tA[:, 0:256].rearrange("p (u t) -> p u t", t=C).unsqueeze(2)
                     .to_broadcast([P, KC * 2, 2, C])).then_inc(s["xT"], 1)

            def ev_k(m, par):
                act.wait_ge(s["khTp"], m + 1)
                copy(Kt[:, :], QK[:, 0:HID]).then_inc(s["Kt"], 1)

            def ev_o(m, par):
                act.wait_ge(s["oTp"], m + 1)
                copy(oT[:, :, :].rearrange("p c t -> p (c t)"), tA[:, 256:512]).then_inc(s["oT"], 1)

            def ev_low(m, par):
                act.wait_ge(s["lowp"], m + 1)
                copy(low[0:LOWR, :], QK[0:LOWR, 0:P]).then_inc(s["low"], 1)

            def ev_v(m, par):
                act.wait_ge(s["Vp"], m + 1)
                v = VO[:, :].rearrange("p (u n) -> p u n", n=2 * D)
                for h in range(2):
                    copy(Vbd[par][h * C:(h + 1) * C, :, h * D:(h + 1) * D], v[h * C:(h + 1) * C, :, h * D:(h + 1) * D])
                for c in range(2):
                    last = copy(Vz[par][c * C:(c + 1) * C, c, :], VO[c * C:(c + 1) * C, c * HID:(c + 1) * HID])
                last.then_inc(s["V"], 1)

            def soft(m, par):
                act.wait_ge(s["zp"], m + 1)
                act.activation(z_abs[:, :], tB[:, :], ACT.Abs).then_inc(s["absd"], 1)
                act.wait_ge(s["absd"], m + 1)
                act.activation(z_exp[:, :], z_abs[:, :], ACT.Exp, scale=-1.0).then_inc(s["expd"], 1)
                act.wait_ge(s["expd"], m + 1)
                if alive(m - 1, NT):
                    act.wait_ge(s["gk"], m)
                act.activation(z_ln[:, :], z_exp[:, :], ACT.Ln, bias=ones[:, 0:1]).then_inc(s["lnd"], 1)

            def ln_std(m, par):
                act.wait_ge(s["mv"], m + 1)
                act.activation(v_ln[:, :], mv[:, 1:2], ACT.Ln, bias=eps_col).then_inc(s["vl"], 1)
                act.wait_ge(s["vl"], m + 1)
                act.activation(rstd[:, :], v_ln[:, :], ACT.Exp, scale=-0.5).then_inc(s["rst"], 1)

            def decays(m, par):
                act.wait_ge(s["gk"], m + 1)
                act.activation(sigm[:, :], lsg[:, HID:2 * HID], ACT.Exp).then_inc(s["sigm"], 1)
                act.wait_ge(s["Dc"], m + 1)
                d = Dc[:, :, :].rearrange("p u s -> p (u s)")
                act.activation(EQ[:, :], d, ACT.Exp, scale=1.0 / GLN)
                act.activation(EK[:, :], d, ACT.Exp, scale=-1.0 / GLN).then_inc(s["ex"], 1)
                act.activation(fa[par][:, :], gk[:, :, 0], ACT.Exp, scale=1.0 / GLN)
                act.activation(fb[par][:, :], Dc[:, :, C - 1], ACT.Exp, scale=1.0 / GLN).then_inc(s["ab"], 1)

            def ev_x1(m, par):
                act.wait_ge(s["x1Tp"], m + 1)
                if alive(m - 1, NT):
                    act.wait_ge(s["x1Tc"], m)
                copy(x1T[:, :, :].rearrange("p c t -> p (c t)"), X7[:, 0:256]).then_inc(s["x1T"], 1)

            def spread_q(m, par):
                act.wait_ge(s["qh"], m + 1)
                for j in range(2):
                    r = slice(32 * j, 32 * j + 32)
                    last = copy(Qbd[r, :, j, :], Qh[par][r, :, :].rearrange("p g (c t) -> p (g c) t", c=2))
                last.then_inc(s["qbd"], 1)

            def softmax(m, par):
                act.wait_ge(s["nmx"], m + 1)
                act.activation(e64[:, :], lg[:, :], ACT.Exp, bias=nmx[:, :], accum_out=esum[:, :])
                act.activation(e8[:, :], mx8[:, :], ACT.Exp, bias=nmx[:, :]).then_inc(s["es"], 1)

            act.dma_start(wo[:, :, :], Wo.rearrange("(c p) n -> p c n", p=P)).then_inc(s["raw"], 16)
            act.dma_start(raw_g[:, :], gate_w).then_inc(s["raw"], 16)
            for t, w in zip(raw_s, (sg_w, su_w)):
                act.dma_start(t[:, :, :], w.rearrange("(m p) n -> p m n", p=I)).then_inc(s["raw"], 16)
            act.dma_start(raw_d[:, :, :], sd_w.rearrange("(c p) n -> p c n", p=P)).then_inc(s["raw"], 16)
            act.wait_ge(s["cst"], 16)
            act.wait_ge(s["low1"], 1)
            act.wait_ge(s["pre"], 10)

            def shared_step(m, par):
                if alive(m, NT):
                    act.wait_ge(s["sgp"], m + 1)
                    if alive(m - 2, NT):
                        act.wait_ge(s["shh"], m - 1)
                    g = SHb[par][0:I, :].rearrange("p (a n t) -> p a n t", a=SM, n=2)
                    act.activation(sh_g[par][:, :, :], g[:, :, 0, :], ACT.Silu).then_inc(s["sil"], 1)
            def tile_step(i, par):
                now, nxt, prev = alive(i, NT), alive(i + 1, NT), alive(i - 1, NT)
                at_end = isinstance(i, int) and i >= NT
                if prev:
                    ev_o(i - 1, 1 - par)
                if at_end:
                    shared_step(2 * (i - NT), 0)
                if nxt:
                    ev_low(i + 1, 1 - par)
                    ev_v(i + 1, 1 - par)
                    soft(i + 1, 1 - par)
                if prev:
                    ln_std(i - 1, 1 - par)
                if nxt:
                    decays(i + 1, 1 - par)
                if at_end:
                    shared_step(2 * (i - NT) + 1, 1)
                if alive(i - 2, NT):
                    softmax(i - 2, par)
                if now:
                    gate_in(i, par)
                if nxt:
                    spread_q(i + 1, 1 - par)
                if now:
                    rms(i, par)
                if alive(i + 2, NT):
                    ev_x(i + 2, par)
                if prev:
                    ev_x1(i - 1, 1 - par)
                if nxt:
                    ev_k(i + 1, 1 - par)
            run_tiles(act, tile_step)

            run_shared(act, shared_step)

            def pair_step(p, k, h):
                if alive(p, NP):
                    act.wait_ge(s["xtp"], p + 1)
                    if alive(p - 2, NP):
                        act.wait_ge(s["gu"], p - 1)
                    copy(gxT[:, k % 2, :], XTb[k % 2][:, 0:HID]).then_inc(s["xt"], 1)
                if alive(p - 1, NP):
                    q = (k - 1) % 2
                    act.wait_ge(s["gu"], p)
                    if alive(p - 3, NP):
                        act.wait_ge(s["hid"], p - 2)
                    act.activation(sg[:, q, :], GUb[q][0:I, 0:P], ACT.Silu).then_inc(s["sig"], 1)
                if alive(p - 2, NP):
                    q, r = k % 2, (k - 2) % GXR
                    act.wait_ge(s["dn"], p - 1)
                    act.wait_ge(s["wd"], p - 1)
                    act.wait_ge(d_put[r], put_done(k - 2 - GXR, h))
                    act.activation(eo[r][:, :], DNb[q][:, 0:HID], ACT.Copy, scale=wsel[:, r:r + 1]).then_inc(s["ev"], 1)
            run_pairs(act, pair_step)

            act.preload_act_table_set("natural_log_exp_and_others")

            def final_std(m):
                act.wait_ge(s["mvf"], m + 1)
                act.activation(vf_ln[:, :], mvf[:, 1:2], ACT.Ln, bias=eps_col).then_inc(s["vfl"], 1)
                act.wait_ge(s["vfl"], m + 1)
                act.activation(rstdf[:, :], vf_ln[:, :], ACT.Exp, scale=-0.5).then_inc(s["rsf"], 1)
            with act.Fori(0, NT) as m:
                final_std(m)

        @block.vector
        def _(dve):
            dve.wait_ge(s["cst"], 16)
            dve.wait_ge(s["pre"], 10)

            def keep_weights():
                dve.wait_ge(s["rawT"], 1)
                dve.tensor_copy(gwT[:, :, :].rearrange("p c e -> p (c e)"), tA[:, 256:256 + KC * E]).then_inc(s["rawE"], 1)
                for n, bank in enumerate((VO, PX)):
                    dve.tensor_copy(sT[n][:, :, :].rearrange("p c i -> p (c i)"), bank[:, 0:KC * SI]).then_inc(s["rawE"], 1)
                dve.tensor_copy(sdT[:, :, :].rearrange("p m h -> p (m h)"), X7[0:I, :]).then_inc(s["rawE"], 1)
                dve.wait_ge(s["nw"], 16 * (P // D))
                for c in range(KC):
                    dve.tensor_scalar(wo[:, c, :], wo[:, c, :], nw_col[:, 0:1], None, ALU.mult).then_inc(s["wo_ready"], 1)

            def squares(m, par):
                dve.wait_ge(s["sq"], m + 1)
                dve.tensor_reduce(ms[:, :], sq[:, :].rearrange("p (h d) -> p h d", d=D), AX.X, ALU.add).then_inc(s["ms"], 1)

            def gated(m, par):
                dve.wait_ge(s["rs"], m + 1)
                dve.tensor_tensor(on[:, :].rearrange("p (h d) -> p h d", d=D),
                                  OG[:, 0:HID].rearrange("p (h d) -> p h d", d=D),
                                  rs[:, :].unsqueeze(2).to_broadcast([P, H, D]), ALU.mult).then_inc(s["on"], 1)
                dve.wait_ge(s["on"], m + 1)
                dve.tensor_tensor(of[:, :], on[:, :], sgate[par][:, :], ALU.mult).then_inc(s["of"], 1)

            def causal(m, par):
                dve.wait_ge(s["sc"], m + 1)
                dve.nop(nofuse=True)
                dve.copy_predicated(Am[:, :, :, :], caus.unsqueeze(1).unsqueeze(1).to_broadcast([P, 4, 4, C]),
                                    SC[:, :, :].rearrange("p u (j t) -> p u j t", t=C)).then_inc(s["am"], 1)

            def post_sum(m, par):
                if first(m):
                    dve.wait_ge(s["xall"], 16)
                dve.wait_ge(s["Wop"], m + 1)
                dve.tensor_tensor(y[:, :], x_all[:, bass.ds(m, 1), :].rearrange("p a h -> p (a h)"), tA[:, 0:HID],
                                  ALU.add).then_inc(s["y"], 1)
                dve.wait_ge(s["y"], m + 1)
                dve.bn_stats(bn6[:, :], y[:, :]).then_inc(s["bn"], 1)
                dve.wait_ge(s["bn"], m + 1)
                dve.nop(nofuse=True)
                dve.bn_aggr(mv[:, :], bn6[:, :]).then_inc(s["mv"], 1)

            def post_norm(m, par):
                dve.wait_ge(s["rst"], m + 1)
                if alive(m - 2, NT):
                    dve.wait_ge(s["x1c"], m - 1)
                dve.tensor_scalar(x1s[par][:, :], y[:, :], mv[:, 0:1], rstd[:, :], ALU.subtract, ALU.mult)\
                    .then_inc(s["x1"], 1)

            def states(m, par):
                slot = m + m // TPB
                u_in = Sst[:, bass.ds(slot, 1), :].rearrange("p a (g n) -> p (a g) n", g=KC)
                u_out = Sst[:, bass.ds(slot + 1, 1), :].rearrange("p a (g n) -> p (a g) n", g=KC)
                dve.wait_ge(s["ab"], m + 1)
                for c in range(2):
                    a = fa[par][:, :].rearrange("p (g c) -> p c g", c=2)[:, c, :]
                    b = (fb[par] if c else fb[1 - par])[:, :].rearrange("p (g c) -> p c g", c=2)[:, 1 - c, :]
                    dve.tensor_tensor(fc[:, c, :], a, b, ALU.mult).then_inc(s["fc"], 1)
                if alive(m - 1, NT):
                    dve.wait_ge(s["U"], 2 * m)
                    dve.wait_ge(s["og"], m)
                dve.wait_ge(s["fc"], 2 * m + 2)
                for c, src, dst in ((0, u_in, Umid[:, :, :]), (1, Umid[:, :, :], u_out)):
                    if c:
                        dve.wait_ge(s["U"], 2 * m + 1)
                    for g in range(KC):
                        last = dve.scalar_tensor_tensor(Tst[c][:, g, :], src[:, g, :], fc[:, c, g:g + 1], blk,
                                                        ALU.mult, ALU.mult)
                    last.then_inc(s[f"T{c}"], 1)
                    dve.wait_ge(s[f"T{c}"], m + 1)
                    dve.wait_ge(s["Pp"], m + 1)
                    dve.tensor_tensor(dst, PX[:, :].rearrange("p (g c n) -> p g c n", g=KC, c=2)[:, :, c, :],
                                      Tst[c][:, :, :], ALU.add).then_inc(s["U"], 1)

            def decay(m, par):
                dve.wait_ge(s["lnd"], m + 1)
                dve.scalar_tensor_tensor(lsg[:, :], tB[:, :], 0.0, z_ln[:, :], ALU.min, ALU.subtract).then_inc(s["gk"], 1)
                dve.wait_ge(s["gk"], m + 1)
                dve.tensor_tensor_scan(Dc[:, :, :].rearrange("p u s -> p (u s)"), lsg[:, 0:HID], scan_keep, 0.0,
                                       ALU.add, ALU.mult).then_inc(s["Dc"], 1)

            def decayed(m, par):
                dve.wait_ge(s["qk"], m + 1)
                dve.wait_ge(s["ex"], m + 1)
                dve.tensor_tensor(Kh[:, :, :].rearrange("p g t -> p (g t)"), QK[:, HID:2 * HID], EK[:, :], ALU.mult)\
                    .then_inc(s["kh"], 1)
                dve.scalar_tensor_tensor(Qh[par][:, :, :].rearrange("p g t -> p (g t)"), QK[:, 0:HID], D ** -0.5,
                                         EQ[:, :], ALU.mult, ALU.mult).then_inc(s["qh"], 1)
                dve.wait_ge(s["kh"], m + 1)
                for h in range(2):
                    last = dve.tensor_scalar(Kbd[:, :, h, :], Kh[:, :, :].rearrange("p g (c t) -> p (g c) t", c=2),
                                             cst[:, C_PAR + h:C_PAR + h + 1], None, ALU.mult)
                last.then_inc(s["kbd"], 1)
                dve.wait_ge(s["qh"], m + 1)
                for j in range(2, 4):
                    r = slice(32 * j, 32 * j + 32)
                    last = dve.tensor_copy(Qbd[r, :, j, :], Qh[par][r, :, :].rearrange("p g (c t) -> p (g c) t", c=2))
                last.then_inc(s["qbd"], 1)
                dve.wait_ge(s["sigm"], m + 1)
                dve.tensor_tensor(sgate[par][:, :], tB[:, HID:2 * HID], sigm[:, :], ALU.mult).then_inc(s["sgt"], 1)

            def route(m, par):
                dve.wait_ge(s["lgp"], m + 1)
                dve.tensor_copy(lg[:, :], X7[:, HID:HID + E]).then_inc(s["lg"], 1)
                dve.wait_ge(s["lg"], m + 1)
                dve.nop(nofuse=True)
                dve.max(mx8[:, :], lg[:, :]).then_inc(s["mx"], 1)
                dve.wait_ge(s["mx"], m + 1)
                dve.tensor_scalar(nmx[:, :], mx8[:, 0:1], -1.0, None, ALU.mult).then_inc(s["nmx"], 1)
                dve.max_index(ix8[:, :], mx8[:, :], lg[:, :]).then_inc(s["ix"], 1)
                dve.wait_ge(s["ix"], m + 1)
                dve.tensor_copy(idx_f[:, :], ix8[:, 0:K]).then_inc(s["idx"], 1)
                dve.wait_ge(s["idx"], m + 1)
                dve.tensor_tensor(oh[:, :, :], eiota.unsqueeze(1).to_broadcast([P, K, E]),
                                  idx_f[:, :].unsqueeze(2).to_broadcast([P, K, E]), ALU.is_equal).then_inc(s["oh"], 1)
                dve.wait_ge(s["oh"], m + 1)
                dve.tensor_reduce(sel[:, :], oh[:, :, :].rearrange("p k e -> p e k"), AX.X, ALU.add).then_inc(s["sel"], 1)

            def place(m, par):
                dve.wait_ge(s["es"], m + 1)
                dve.reciprocal(erec[:, :], esum[:, :]).then_inc(s["rec"], 1)
                dve.wait_ge(s["cum"], m + 1)
                dve.tensor_tensor(pm[:, :, :], PX[:, 0:E].unsqueeze(1).to_broadcast([P, K, E]), oh[:, :, :],
                                  ALU.mult).then_inc(s["pm"], 1)
                dve.tensor_tensor(sel_acc[:, :], sel_acc[:, :], sel[:, :], ALU.add).then_inc(s["acc"], 1)
                dve.wait_ge(s["rec"], m + 1)
                if alive(m - 2, NT):
                    dve.wait_ge(d_scat[par], half(m - 2, par, K * 16))
                dve.tensor_scalar(rows[par][:, WCOL:WCOL + K], e8[:, 0:K], erec[:, :], None, ALU.mult)
                dve.tensor_copy(rows[par][:, ICOL:ICOL + K], idx_f[:, :])
                dve.tensor_copy(rows[par][:, DCOL:DCOL + K], cst[:, bass.ds(C_D + m * K, K)]).then_inc(s["wr"], 1)
                dve.wait_ge(s["pm"], m + 1)
                dve.tensor_reduce(pos[:, :], pm[:, :, :], AX.X, ALU.add).then_inc(s["pos"], 1)
                dve.wait_ge(s["pos"], m + 1)
                dve.tensor_scalar(over[:, :], pos[:, :], CAP - 0.5, float(NOWHERE), ALU.is_ge, ALU.mult)
                dve.scalar_tensor_tensor(slot_f[:, :], idx_f[:, :], float(CAP), pos[:, :], ALU.mult, ALU.add).then_inc(s["sf"], 1)
                dve.wait_ge(s["sf"], m + 1)
                dve.tensor_tensor(slot_u[par][:, :], slot_f[:, :], over[:, :], ALU.add).then_inc(s["slot"], 1)

            def shared_step(m, par):
                if alive(m, NT):
                    dve.wait_ge(s["sil"], m + 1)
                    if alive(m - 2, NT):
                        dve.wait_ge(s["sdp"], m - 1)
                    u = SHb[par][0:I, :].rearrange("p (a n t) -> p a n t", a=SM, n=2)
                    dve.tensor_tensor(sh_h[par][:, :, :], sh_g[par][:, :, :], u[:, :, 1, :], ALU.mult).then_inc(s["shh"], 1)
                if alive(m - 1, NT):
                    dve.wait_ge(s["sdp"], m)
                    dve.wait_ge(s["xrow"], m)
                    dve.tensor_tensor(base[:, bass.ds(m - 1, 1), :].rearrange("p a h -> p (a h)"),
                                      x1_all[:, bass.ds(m - 1, 1), :].rearrange("p a h -> p (a h)"),
                                      SDb[1 - par], ALU.add).then_inc(s["base"], 1)

            def tile_step(i, par):
                now, nxt, prev = alive(i, NT), alive(i + 1, NT), alive(i - 1, NT)
                at_end = isinstance(i, int) and i >= NT
                if now:
                    states(i, par)
                if alive(i - 2, NT):
                    route(i - 2, par)
                if at_end:
                    shared_step(2 * (i - NT), 0)
                if prev:
                    post_sum(i - 1, 1 - par)
                if nxt:
                    decay(i + 1, 1 - par)
                if prev:
                    post_norm(i - 1, 1 - par)
                if nxt:
                    decayed(i + 1, 1 - par)
                if now:
                    squares(i, par)
                if at_end:
                    shared_step(2 * (i - NT) + 1, 1)
                if alive(i - 2, NT):
                    place(i - 2, par)
                if now:
                    gated(i, par)
                if nxt:
                    causal(i + 1, 1 - par)
                if isinstance(i, int) and i == -1:
                    keep_weights()
            run_tiles(dve, tile_step)
            run_shared(dve, shared_step)

            def pair_step(p, k, h):
                if alive(p, NP):
                    r = k % GXR
                    dve.wait_ge(d_gx[r], slot_loads(k, h))
                    dve.wait_ge(d_put[r], put_done(k - GXR, h))
                    ecol = cst[:, bass.ds(C_ECOL + p, 1)]
                    dve.scalar_tensor_tensor(junk[:, :], gx[:, r, ICOL:ICOL + K], ecol, gx[:, r, WCOL:WCOL + K],
                                             ALU.is_equal, ALU.mult, accum_out=wsel[:, r:r + 1]).then_inc(s["wd"], 1)
                    dve.wait_ge(s["wd"], p + 1)
                    dve.scalar_tensor_tensor(junk[:, :], gx[:, r, ICOL:ICOL + K], ecol, gx[:, r, DCOL:DCOL + K],
                                             ALU.is_equal, ALU.mult, accum_out=dsel[:, r:r + 1]).then_inc(s["dsel"], 1)
                    dve.wait_ge(s["dsel"], p + 1)
                    dve.tensor_scalar(dest[r][:, :], dsel[:, r:r + 1], float(NOWHERE), None, ALU.add).then_inc(s["dest"], 1)
                if alive(p - 1, NP):
                    q = (k - 1) % 2
                    dve.wait_ge(s["sig"], p)
                    if alive(p - 3, NP):
                        dve.wait_ge(s["dn"], p - 2)
                    dve.tensor_tensor(hid[:, q, :], sg[:, q, :], GUb[q][0:I, P:2 * P], ALU.mult).then_inc(s["hid"], 1)
            run_pairs(dve, pair_step)

            def halves(m):
                dve.wait_ge(d_cin[m], 16)
                if m >= 2:
                    dve.wait_ge(s["csp"], m - 1)
                dve.tensor_tensor(half_sum[m % 2][:, :], cin[m][:, 0:K // 2 * HID], cin[m][:, K // 2 * HID:K * HID], ALU.add)\
                    .then_inc(s["hsum"], 1)

            def finish(m, par):
                dve.wait_ge(s["csp"], m + 1)
                dve.bn_stats(bnf[:, :], CSb[par]).then_inc(s["bnf"], 1)
                dve.wait_ge(s["bnf"], m + 1)
                dve.bn_aggr(mvf[:, :], bnf[:, :]).then_inc(s["mvf"], 1)
                dve.wait_ge(s["rsf"], m + 1)
                if m >= 2:
                    dve.wait_ge(d_out[par], half(m - 2, par, 16))
                dve.tensor_scalar(res[par][:, :], CSb[par], mvf[:, 0:1], rstdf[:, :], ALU.subtract, ALU.mult)\
                    .then_inc(s["res"], 1)
            halves(0)
            for m in range(NT):
                if m + 1 < NT:
                    halves(m + 1)
                finish(m, m % 2)



_INS = ["L0_attn_x", "L0_attn_Wq", "L0_attn_Wk", "L0_attn_Wv", "L0_attn_Wg1", "L0_attn_Wg2", "L0_attn_bg2",
        "L0_attn_Wgate", "L0_attn_norm_w", "L0_attn_Wo", "L0_ffn_gate_w", "L0_ffn_gate_up_proj", "L0_ffn_down_proj",
        "L0_ffn_shared_gate_w", "L0_ffn_shared_up_w", "L0_ffn_shared_down_w"]


def kernel(**inputs):
    import concourse.bacc as bacc
    from concourse.bass_utils import run_bass_kernel_spmd

    nc = bacc.Bacc("TRN2", target_bir_lowering=False, num_devices=1)
    arrays = {"consts": constants()}
    args = [nc.dram_tensor("consts", arrays["consts"].shape, F32, kind="ExternalInput").ap()]
    for name in _INS:
        a = np.ascontiguousarray(inputs[name])
        arrays[f"in_{name}"] = a
        args.append(nc.dram_tensor(f"in_{name}", a.shape, mybir.dt.from_np(a.dtype), kind="ExternalInput").ap())
    args.append(nc.dram_tensor("result", (B, L, HID), F32, kind="ExternalOutput").ap())
    build(nc, *args)
    r = run_bass_kernel_spmd(nc, [arrays], core_ids=[0])
    return r.results[0]["result"]
```

```python
from contextlib import ExitStack

import numpy as np

import concourse.bass as bass
import concourse.mybir as mybir

F32 = mybir.dt.float32
U32 = mybir.dt.uint32
I32 = mybir.dt.int32
ALU = mybir.AluOpType
ACT = mybir.ActivationFunctionType
AX = mybir.AxisListType

P = 128
B, L, HID = 2, 512, 256
T = B * L
NT = T // P
TPB = L // P
KC = HID // P
H, D = 16, 16
C = 64
LOWR = 16
GLN = 16.0
EPS = 1e-5
E, K, CAP = 64, 6, 64
I = 96
SI = 192
SM = SI // I
NP = E // 2
ROW = HID + 3 * K
WCOL, ICOL, DCOL = HID, HID + K, HID + 2 * K
NOWHERE = 8192
RING = 12
GXR = 6
HEAD, TAIL = 4, 6
RING_FIRST, RING_END = HEAD - 2, NP - TAIL + 1
FIRST = RING_FIRST + RING
EXTRA = NP - RING_END

C_ID, C_BLK, C_TRI, C_ONE, C_CAUS, C_SCAN, C_EI, C_D, C_ECOL, C_PAR, C_EPS, C_END = np.cumsum(
    [0, P, P, P, P, C, KC * P, E, NT * K, NP, 2, 1]).tolist()


def constants():
    c = np.zeros((P, C_END), np.float32)
    p = np.arange(P)
    c[:, C_ID:C_ID + P] = np.eye(P)
    c[:, C_BLK:C_BLK + P] = p[:, None] // D == p[None, :] // D
    c[:, C_TRI:C_TRI + P] = p[:, None] < p[None, :]
    c[:, C_ONE:C_ONE + P] = 1.0
    c[:, C_CAUS:C_CAUS + C] = p[:, None] % C <= np.arange(C)[None, :]
    c[:, C_SCAN:C_SCAN + KC * P] = np.arange(KC * P) % C != 0
    c[:, C_EI:C_EI + E] = np.arange(E)
    token = np.arange(NT)[None, :, None] * P + p[:, None, None]
    c[:, C_D:C_D + NT * K] = (token * K + np.arange(K)[None, None, :] - NOWHERE).reshape(P, NT * K)
    c[:, C_ECOL:C_ECOL + NP] = 2 * np.arange(NP)[None, :] + p[:, None] // C
    c[:, C_PAR:C_PAR + 2] = (p[:, None] // D) % 2 == np.arange(2)[None, :]
    c[:, C_EPS] = EPS
    return c


def alive(m, n):
    return not isinstance(m, int) or 0 <= m < n


def weight_place(p):
    return p if p < FIRST else RING_FIRST + (p - RING_FIRST) % RING if p < RING_END else p - RING_END + FIRST


def first(m):
    return isinstance(m, int) and m == 0


def build(nc, consts, x, Wq, Wk, Wv, Wg1, Wg2, bg2, Wgate, norm_w, Wo, gate_w, gup, down, sg_w, su_w, sd_w, out):
    slots = nc.dram_tensor("slot_rows", [E * CAP, ROW], F32, kind="Internal").ap()
    parts = nc.dram_tensor("choice_rows", [T * K, HID], F32, kind="Internal").ap()
    x_rows = x.rearrange("b (t p) h -> (b t) p h", p=P)
    out_rows = out.rearrange("b (t p) h -> (b t) p h", p=P)

    with ExitStack() as ctx:
        def sb(name, shape, dt=F32):
            return ctx.enter_context(nc.sbuf_tensor(name, shape, dt))

        def ps(name, shape):
            return ctx.enter_context(nc.psum_tensor(name, shape, F32))

        def sem(name):
            return ctx.enter_context(nc.semaphore(name))

        def views(region, *shapes):
            at, out = 0, []
            for shape in shapes:
                n, axes = int(np.prod(shape)), "abc"[:len(shape)]
                v = region[:, at:at + n]
                if len(shape) > 1:
                    v = v.rearrange(f"p ({' '.join(axes)}) -> p {' '.join(axes)}", **dict(zip(axes, shape)))
                out.append(v)
                at += n
            return out

        cst = sb("cst", [P, C_END])
        ident, blk, tri, ones = (cst[:, a:a + P] for a in (C_ID, C_BLK, C_TRI, C_ONE))
        caus = cst[:, C_CAUS:C_CAUS + C].bitcast(I32)
        scan_keep = cst[:, C_SCAN:C_SCAN + KC * P]
        eiota = cst[:, C_EI:C_EI + E]
        eps_col = cst[:, C_EPS:C_EPS + 1]
        wgu_r = sb("wgu_r", [P, FIRST + EXTRA, 2 * KC, 2 * I])
        wdn_r = sb("wdn_r", [P, FIRST + EXTRA, 2, HID])
        wq, wk, wv, Qbd, Am = views(wgu_r[:, FIRST:, :, :].rearrange("p r a n -> p (r a n)"),
                                    *[(KC, HID)] * 3, (KC * 2, 4, C), (4, 4, C))
        *V2, Kh, Kt = views(wdn_r[:, FIRST:, :, :].rearrange("p r a n -> p (r a n)"),
                            *[(16, 2 * D)] * 2, *[(2, HID)] * 2, (KC, P), (HID,))
        Vbd, Vz = V2[:2], V2[2:]
        wg, wo = (sb(n, [P, KC, HID]) for n in ("wg", "wo"))
        wg1 = sb("wg1", [P, KC, LOWR])
        wg2 = sb("wg2", [LOWR + 1, HID])
        nw_col = sb("nw_col", [P, 1])
        raw_g = sb("raw_g", [E, HID])
        raw_s = [sb(n, [I, SM, HID]) for n in ("raw_sg", "raw_su")]
        raw_d = sb("raw_d", [P, KC, SI])
        gwT = sb("gwT", [P, KC, E])
        sT = [sb(n, [P, KC, SI]) for n in ("sgT", "suT")]
        sdT = sb("sdT", [I, SM, HID])
        late = sb("late", [P, NT * HID])
        x_all = late[:, 0:NT * HID].rearrange("p (t h) -> p t h", t=NT)
        gx = late[:, 0:GXR * ROW].rearrange("p (g n) -> p g n", g=GXR)
        x_in = [sb(f"x_in{b}", [P, HID]) for b in range(2)]
        xT = sb("xT", [P, KC, P])
        xTd = sb("xTd", [P, KC * 2, 2, C])
        low = sb("low", [LOWR + 1, P])
        soft = sb("soft", [P, 4, 2 * HID])
        z_abs, z_exp, z_ln, lsg = (soft[:, n, :] for n in range(4))
        gk = lsg[:, 0:HID].rearrange("p (u s) -> p u s", s=C)
        sigm = sb("sigm", [P, HID])
        Dc = sb("Dc", [P, KC * 2, C])
        EQ = sb("EQ", [P, KC * P])
        EK = sb("EK", [P, KC * P])
        fa = [sb(f"fa{b}", [P, KC * 2]) for b in range(2)]
        fb = [sb(f"fb{b}", [P, KC * 2]) for b in range(2)]
        Qh = [sb(f"Qh{b}", [P, KC, P]) for b in range(2)]
        Kbd = sb("Kbd", [P, KC * 2, 2, C])
        Tst = [sb(f"Tst{c}", [P, KC, P]) for c in range(2)]
        Umid = sb("Umid", [P, KC, P])
        fc = [sb(f"fc{b}", [P, 2, KC]) for b in range(2)]
        Sst = sb("Sst", [P, NT + B, KC * P])
        sq = sb("sq", [P, HID])
        ms = sb("ms", [P, H])
        ms_ln = sb("ms_ln", [P, H])
        rs = sb("rs", [P, H])
        sgate = [sb(f"sgate{b}", [P, HID]) for b in range(2)]
        on = sb("on", [P, HID])
        of = sb("of", [P, HID])
        oT = sb("oT", [P, KC, P])
        y = sb("y", [P, HID])
        ysum = sb("ysum", [P, 1])
        nmean = sb("nmean", [P, 1])
        dev2 = sb("dev2", [P, HID])
        vsum = sb("vsum", [P, 1])
        v_ln = sb("v_ln", [P, 1])
        rstd = sb("rstd", [P, 1])
        x1s = [sb(f"x1s{b}", [P, HID]) for b in range(2)]
        x1T = sb("x1T", [P, KC, P])
        x1_all = sb("x1_all", [P, NT, HID])
        rows = [sb(f"rows{b}", [P, ROW]) for b in range(2)]
        idx_f = sb("idx_f", [P, K])
        x1T_all = sb("x1T_all", [P, NT, KC * P])
        lg = sb("lg", [P, E])
        mx8 = sb("mx8", [P, 8])
        ix8 = sb("ix8", [P, 8], U32)
        nmx = sb("nmx", [P, 1])
        e64 = sb("e64", [P, E])
        e8 = sb("e8", [P, 8])
        esum = sb("esum", [P, 1])
        erec = sb("erec", [P, 1])
        oh = sb("oh", [P, K, E])
        sel = sb("sel", [P, E])
        sel_acc = sb("sel_acc", [P, E])
        pm = sb("pm", [P, K, E])
        pos = sb("pos", [P, K])
        over = sb("over", [P, K])
        slot_f = sb("slot_f", [P, K])
        slot_u = [sb(f"slot_u{b}", [P, K], U32) for b in range(2)]
        filler = sb("filler", [P, 2, ROW])
        zeros = sb("zeros", [P, 3 * HID])
        gxT = Sst[:, 0:2, :]
        sg = Sst[:, 2, 0:2 * I].rearrange("p (a n) -> p a n", a=2)
        hid = Sst[:, 3, 0:2 * I].rearrange("p (a n) -> p a n", a=2)
        hidT = Sst[0:I, 4, :].rearrange("p (a t) -> p a t", a=2)
        junk = sb("junk", [P, K])
        wsel = sb("wsel", [P, GXR])
        dsel = sb("dsel", [P, GXR])
        dest = [sb(f"dest{b}", [P, 1], U32) for b in range(GXR)]
        eo = [soft[:, b // 2, b % 2 * HID:(b % 2 + 1) * HID] for b in range(GXR)]
        sh_g = [sb(f"sh_g{b}", [I, SM, P]) for b in range(2)]
        sh_h = [sb(f"sh_h{b}", [I, SM, P]) for b in range(2)]
        base = x1_all
        cin = [wgu_r[:, 2 * m:2 * m + 2, :, :].rearrange("p a b n -> p (a b n)") for m in range(NT)]
        half_sum = [x1T_all[:, b * K // 2:(b + 1) * K // 2, :].rearrange("p a n -> p (a n)") for b in range(2)]
        bnf = sb("bnf", [P, 6])
        mvf = sb("mvf", [P, 2])
        vf_ln = sb("vf_ln", [P, 1])
        rstdf = sb("rstdf", [P, 1])
        res = [Sst[:, m, :] for m in range(NT)]

        tA, tB, QK, VO, PX, X7 = (ps(n, [P, 512]) for n in ("tA", "tB", "QK", "VO", "PX", "X7"))
        SC = ps("SC", [P, 4, 4 * C])
        SCb = SC[:, :, :].rearrange("p (b u) n -> p b (u n)", b=2)
        OG = VO
        XTb, GUb, DNb = (tA, tB), (QK, VO), (PX, X7)
        HTb = (SC[:, 0, :], SC[:, 2, :])

        SHb = (QK, tB)
        SDb = (SC[:, 0, :], SC[:, 2, :])
        CSb = (*SDb, QK, VO)

        s = {}
        for n in ("ident cst w_low w_val w_gate w_qk w_out raw nw xall fill zero pre prefilled wo_ready low1 "
                  "rawT rawE xTp xT lowp low Vp V zp qk absd expd lnd gk Dc ex ab kh qh kbd khTp Kt sc am fc Pp T0 T1 U "
                  "og sq sigm qbd ms msl rs sgt on of oTp oT Wop y mv vs vl rst x1 x1Tp x1T x1c x1Tc lgp lg mx ix nmx es idx oh "
                  "sel wr cum acc pm pos sf slot xrow rec "
                  "xtp xt gu sig hid hTp hT dn ev wd dsel dest "
                  "sgp sil shh sdp base hsum csp bnf mvf vfl rsf res").split():
            s[n] = sem("s_" + n)
        d_xin = [sem(f"d_xin{b}") for b in range(2)]
        d_scat = [sem(f"d_scat{b}") for b in range(2)]
        d_w = [sem(f"d_w{k}") for k in range(FIRST + EXTRA)]
        d_gx = [sem(f"d_gx{k}") for k in range(GXR)]
        d_put = [sem(f"d_put{k}") for k in range(GXR)]
        d_cin = [sem(f"d_cin{m}") for m in range(NT)]
        d_out = sem("d_out")
        EARLY = range(0, 5)
        LATE = range(5, NT)
        NRAW = 4 * 16

        def half(m, par, per):
            return (m + (1 if par else 2)) * (per // 2)

        def run_tiles(eng, body):
            for i in range(-2, 2):
                body(i, i % 2)
            with eng.Fori(1, NT // 2 - 1) as h:
                body(h * 2, 0)
                body(h * 2 + 1, 1)
            for i in range(NT - 2, NT + 2):
                body(i, i % 2)

        def run_pairs(eng, body):
            for k in range(HEAD):
                body(k, k, 0)
            with eng.Fori(0, (NP + 2 - HEAD - TAIL) // RING) as h:
                for k in range(HEAD, HEAD + RING):
                    body(h * RING + k, k, h)
            for p in range(NP + 2 - TAIL, NP + 2):
                body(p, p, 0)

        def run_shared(eng, body, tiles):
            for m in range(tiles.start, tiles.stop + 1):
                body(m, m < tiles.stop, m > tiles.start)

        def slot_loads(k, h):
            return h * (16 * RING // GXR) + (k // GXR + 1) * 16

        def put_done(k, h):
            return h * (16 * RING // GXR) + (k // GXR + 2) * 16

        def weight_loads(k, h):
            return h * 32 + ((k - RING_FIRST) // RING + 1) * 32 if RING_FIRST <= k < RING_END else 32

        block = ctx.enter_context(nc.Block())

        @block.sync
        def _(sp):
            def load_x(m, par):
                sp.dma_start(x_in[par][:, :], x_rows[m]).then_inc(d_xin[par], 16)

            def load_weight(t, w, n):
                sp.dma_start(t[:, :, :], w.rearrange("(c p) n -> p c n", p=P)).then_inc(s[n], 16)
            sp.dma_start(ident, consts[:, C_ID:C_ID + P]).then_inc(s["ident"], 16)
            load_x(0, 0)
            load_weight(wg1, Wg1, "w_low")
            load_weight(wg, Wgate, "w_gate")
            sp.dma_start(wg2[0:LOWR, :], Wg2).then_inc(s["w_gate"], 16)
            sp.dma_start(wg2[LOWR:LOWR + 1, :], bg2.rearrange("(a n) -> a n", a=1)).then_inc(s["w_gate"], 16)
            sp.dma_start(cst[:, C_ID + P:C_END], consts[:, C_ID + P:C_END]).then_inc(s["cst"], 16)
            load_weight(wq, Wq, "w_qk")
            load_weight(wk, Wk, "w_qk")
            sp.dma_start(raw_g[:, :], gate_w).then_inc(s["raw"], 16)
            for t, w in zip(raw_s, (sg_w, su_w)):
                sp.dma_start(t[:, :, :], w.rearrange("(m p) n -> p m n", p=I)).then_inc(s["raw"], 16)
            sp.dma_start(raw_d[:, :, :], sd_w.rearrange("(c p) n -> p c n", p=P)).then_inc(s["raw"], 16)
            load_weight(wv, Wv, "w_val")
            load_x(1, 1)
            load_weight(wo, Wo, "w_out")
            sp.wait_ge(s["xTp"], 1)
            load_x(2, 0)
            sp.dma_start(x_all[:, :, :], x_rows.rearrange("t p h -> p t h")).then_inc(s["xall"], 16)
            for h in range(P // D):
                sp.dma_start(nw_col[h * D:(h + 1) * D, :], norm_w.rearrange("(d a) -> d a", a=1)).then_inc(s["nw"], 16)

            sp.wait_ge(s["xTp"], 2)
            load_x(3, 1)
            sp.wait_ge(s["fill"], 2)
            sp.dma_start(slots.rearrange("(p a) n -> p a n", p=P),
                          filler[:, 0:1, :].to_broadcast([P, E * CAP // P, ROW])).then_inc(s["prefilled"], 16)

            def load_weights(q):
                at = weight_place(q)
                sp.dma_start(wgu_r[:, at, :, :], gup[2 * q:2 * q + 2].rearrange("e (c p) n -> p (e c) n", p=P))\
                    .then_inc(d_w[at], 16)
                sp.dma_start(wdn_r[0:I, at, :, :], down[2 * q:2 * q + 2].rearrange("e p n -> p e n")).then_inc(d_w[at], 16)

            def load_slots(p):
                sp.dma_start(gx[:, p % GXR, :], slots[p * P:(p + 1) * P]).then_inc(d_gx[p % GXR], 16)

            for m in range(4, NT + 3):
                if m < NT:
                    sp.wait_ge(s["xTp"], m - 1)
                    load_x(m, m % 2)
                else:
                    sp.wait_ge(s["y"], m - 5)
                for q in range(2 * m - 8, 2 * m - 6):
                    load_weights(q)
            sp.wait_ge(s["og"], NT)
            for q in range(RING_END, NP):
                load_weights(q)
            for par in range(2):
                sp.wait_ge(d_scat[par], half(NT - 2 + par, par, K * 16))
            for p in range(GXR):
                load_slots(p)
            q = FIRST
            for p in range(GXR, NP):
                sp.wait_ge(s["xtp"], p - GXR + 1)
                sp.wait_ge(s["dsel"], p - GXR + 1)
                load_slots(p)
                if q < RING_END and p >= FIRST - 3 + (q - FIRST) * 7 // 5:
                    sp.wait_ge(s["dn"], q - RING + 1)
                    load_weights(q)
                    q += 1

            for k in range(GXR):
                sp.wait_ge(d_put[k], 16 * (1 + len(range(k, NP, GXR))))
            for m in range(NT):
                sp.dma_start(cin[m], parts[m * P * K:(m + 1) * P * K].rearrange("(p k) h -> p (k h)", k=K))\
                    .then_inc(d_cin[m], 16)

            for m in range(NT):
                sp.wait_ge(s["res"], m + 1)
                sp.dma_start(out_rows[m], res[m]).then_inc(d_out, 16)
            sp.wait_ge(d_out, 16 * NT)

        @block.gpsimd
        def _(pool):
            pool.memset(low[:, :], 1.0).then_inc(s["low1"], 1)
            pool.memset(filler[:, :, :], 0.0).then_inc(s["fill"], 1)
            pool.wait_ge(s["fill"], 1)
            pool.memset(filler[:, :, ICOL:ICOL + K], -1.0).then_inc(s["fill"], 1)
            pool.memset(zeros[:, :], 0.0).then_inc(s["zero"], 1)
            for b in range(2):
                pool.memset(Vbd[b][:, :, :], 0.0).then_inc(s["pre"], 1)
                pool.memset(Vz[b][:, :, :], 0.0).then_inc(s["pre"], 1)
            pool.memset(Qbd[:, :, :, :], 0.0).then_inc(s["pre"], 1)
            pool.memset(Am[:, :, :, :], 0.0).then_inc(s["pre"], 1)
            pool.memset(fb[1][:, :], 1.0).then_inc(s["pre"], 1)
            pool.memset(sel_acc[:, :], 0.0).then_inc(s["pre"], 1)
            for b in range(B):
                pool.memset(Sst[:, b * (TPB + 1), :], 0.0).then_inc(s["pre"], 1)
            def fill_choice_rows():
                pool.wait_ge(s["zero"], 1)
                pool.wait_ge(s["prefilled"], 16)
                for k in range(GXR):
                    a, b = k * T // P // GXR, (k + 1) * T // P // GXR
                    pool.dma_start(parts.rearrange("(p a) n -> p a n", p=P)[:, a * K:b * K, :].rearrange("p (a b) n -> p a (b n)", b=3),
                                   zeros[:, :].unsqueeze(1).to_broadcast([P, (b - a) * K // 3, 3 * HID])).then_inc(d_put[k], 16)

            def coefficients(m, par):
                pool.wait_ge(s["ab"], m + 1)
                if alive(m - 2, NT):
                    pool.wait_ge(s["T1"], m - 1)
                pool.nop(nofuse=True)
                for c in range(2):
                    a = fa[par][:, :].rearrange("p (g c) -> p c g", c=2)[:, c, :]
                    b = (fb[par] if c else fb[1 - par])[:, :].rearrange("p (g c) -> p c g", c=2)[:, 1 - c, :]
                    pool.tensor_tensor(fc[par][:, c, :], a, b, ALU.mult).then_inc(s["fc"], 1)

            def dispatch(m, par):
                pool.wait_ge(s["xrow"], m + 1)
                pool.wait_ge(s["wr"], m + 1)
                pool.wait_ge(s["slot"], m + 1)
                pool.nop(nofuse=True)
                for k in range(K):
                    pool.indirect_dma_start(slots, bass.IndirectOffsetOnAxis(ap=slot_u[par][:, k:k + 1], axis=0),
                                            rows[par][:, :], None, bounds_check=last_slot,
                                            oob_is_err=False).then_inc(d_scat[par], 16)

            def tile_step(i, par):
                if alive(i + 1, NT):
                    coefficients(i + 1, 1 - par)
                if first(i):
                    fill_choice_rows()
                if alive(i - 2, NT):
                    dispatch(i - 2, par)
            last_slot, last_part = pool.to_reg(E * CAP - 1), pool.to_reg(T * K - 1)
            run_tiles(pool, tile_step)
            for k in range(GXR):
                pool.wait_ge(d_put[k], 16)

            def put(p, k, h):
                if k >= 2:
                    q = (k - 2) % GXR
                    pool.wait_ge(s["dest"], p - 1)
                    pool.wait_ge(s["ev"], p - 1)
                    pool.nop(nofuse=True)
                    pool.indirect_dma_start(parts, bass.IndirectOffsetOnAxis(ap=dest[q][:, :], axis=0),
                                            eo[q][:, :], None, bounds_check=last_part, oob_is_err=False)\
                        .then_inc(d_put[q], 16)
            run_pairs(pool, put)

        @block.tensor
        def _(pe):
            def mm(o, a, b, start, stop=True):
                return pe.matmul(o, a, b, start=start, stop=stop, skip_group_check=True)

            def t_weights():
                pe.wait_ge(s["raw"], NRAW)
                for c in range(KC):
                    pe.transpose(SCb[:, 0, c * E:(c + 1) * E], raw_g[:, c * P:(c + 1) * P], ident[0:E, 0:E])
                for n, bank in enumerate((SCb[:, 1, :], PX)):
                    for c in range(KC):
                        for m in range(SM):
                            pe.transpose(bank[:, c * SI + m * I:c * SI + (m + 1) * I],
                                         raw_s[n][:, m, c * P:(c + 1) * P], ident[0:I, 0:I])
                for m in range(SM):
                    for c in range(KC):
                        last = pe.transpose(X7[0:I, m * HID + c * P:m * HID + (c + 1) * P],
                                            raw_d[:, c, m * I:(m + 1) * I], ident)
                last.then_inc(s["rawT"], 1)

            def t_x(m, par):
                if first(m):
                    pe.wait_ge(s["ident"], 16)
                pe.wait_ge(d_xin[par], half(m, par, 16))
                if alive(m - 3, NT):
                    pe.wait_ge(s["y"], m - 2)
                for c in range(KC):
                    last = pe.transpose(tA[:, c * P:(c + 1) * P], x_in[par][:, c * P:(c + 1) * P], ident)
                last.then_inc(s["xTp"], 1)

            def t_k(m, par):
                pe.wait_ge(s["kh"], m + 1)
                pe.wait_ge(s["qh"], m + 1)
                for c in range(KC):
                    last = pe.transpose(QK[:, c * P:(c + 1) * P], Kh[:, c, :], ident)
                last.then_inc(s["khTp"], 1)

            def scores(m, par):
                pe.wait_ge(s["kbd"], m + 1)
                pe.wait_ge(s["qbd"], m + 1)
                if first(m):
                    pe.wait_ge(s["rawE"], 2)
                if alive(m - 1, NT):
                    pe.wait_ge(s["am"], m)
                for u in range(KC * 2):
                    last = mm(SC[:, u, :], Kbd[:, u, :, :].rearrange("p a s -> p (a s)"),
                              Qbd[:, u, :, :].rearrange("p j s -> p (j s)"), True)
                last.then_inc(s["sc"], 1)

            def t_o(m, par):
                pe.wait_ge(s["of"], m + 1)
                if alive(m + 2, NT):
                    pe.wait_ge(s["xT"], m + 3)
                for c in range(KC):
                    last = pe.transpose(tA[:, 256 + c * P:256 + (c + 1) * P], of[:, c * P:(c + 1) * P], ident)
                last.then_inc(s["oTp"], 1)

            def low_rank(m, par):
                pe.wait_ge(s["xT"], m + 1)
                if first(m):
                    pe.wait_ge(s["w_low"], 16)
                if alive(m - 1, NT):
                    pe.wait_ge(s["kh"], m)
                    pe.wait_ge(s["qh"], m)
                if isinstance(m, int) and m == 1:
                    pe.wait_ge(s["Kt"], m)
                for c in range(KC):
                    last = mm(QK[0:LOWR, HID:HID + P], wg1[:, c, :], xT[:, c, :], c == 0, c == KC - 1)
                last.then_inc(s["lowp"], 1)

            def values(m, par):
                if first(m):
                    pe.wait_ge(s["w_val"], 16)
                if alive(m - 2, NT):
                    pe.wait_ge(s["on"], m - 1)
                for a in range(2):
                    for c in range(KC):
                        last = mm(VO[:, a * HID:(a + 1) * HID], xTd[:, 2 * c + a, :, :].rearrange("p h t -> p (h t)"),
                                  wv[:, c, :], c == 0, c == KC - 1)
                last.then_inc(s["Vp"], 1)

            def output_gate(m, par):
                if alive(m - 1, NT):
                    pe.wait_ge(s["sgt"], m)
                if first(m):
                    pe.wait_ge(s["w_gate"], 3 * 16)
                for c in range(KC):
                    mm(tB[:, HID:2 * HID], xT[:, c, :], wg[:, c, :], c == 0, c == KC - 1)

            def decay_in(m, par):
                pe.wait_ge(s["low"], m + 1)
                for g in range(KC):
                    last = mm(tB[:, g * P:(g + 1) * P], wg2[:, g * P:(g + 1) * P], low[:, :], False)
                last.then_inc(s["zp"], 1)

            def queries_keys(m, par):
                if first(m):
                    pe.wait_ge(s["w_qk"], 2 * 16)
                else:
                    pe.wait_ge(s["Kt"], m)
                for w, o in ((wq, 0), (wk, HID)):
                    for g in range(KC):
                        for c in range(KC):
                            last = mm(QK[:, o + g * P:o + (g + 1) * P], w[:, c, g * P:(g + 1) * P],
                                      xT[:, c, :], c == 0, c == KC - 1)
                last.then_inc(s["qk"], 1)

            def out_proj(m, par):
                pe.wait_ge(s["oT"], m + 1)
                if first(m):
                    pe.wait_ge(s["wo_ready"], 2)
                for c in range(KC):
                    last = mm(tA[:, 0:HID], oT[:, c, :], wo[:, c, :], c == 0, c == KC - 1)
                last.then_inc(s["Wop"], 1)

            def state(m, par):
                pe.wait_ge(s["Kt"], m + 1)
                pe.wait_ge(s["V"], m + 1)
                if first(m):
                    pe.wait_ge(s["rawE"], 4)
                if alive(m - 1, NT):
                    pe.wait_ge(s["U"], 2 * m)
                if alive(m - 3, NT):
                    pe.wait_ge(s["pm"], m - 2)
                for g in range(KC):
                    last = mm(PX[:, g * HID:(g + 1) * HID].rearrange("p (c n) -> p c n", c=2), Kt[:, g * P:(g + 1) * P],
                              Vz[par][:, :, g * P:(g + 1) * P], True)
                last.then_inc(s["Pp"], 1)

            def t_x1(m, par):
                pe.wait_ge(s["x1"], m + 1)
                for c in range(KC):
                    last = pe.transpose(X7[:, c * P:(c + 1) * P], x1s[par][:, c * P:(c + 1) * P], ident)
                last.then_inc(s["x1Tp"], 1)

            def count(m, par):
                pe.wait_ge(s["sel"], m + 1)
                if alive(m - 1, NT):
                    pe.wait_ge(s["acc"], m)
                    pe.wait_ge(s["pm"], m)
                if alive(m + 2, NT):
                    pe.wait_ge(s["U"], 2 * m + 6)
                mm(PX[:, 0:E], tri, sel[:, :], True, False)
                mm(PX[:, 0:E], ones, sel_acc[:, :], False).then_inc(s["cum"], 1)

            def attend(m, par):
                if alive(m + 1, NT):
                    pe.wait_ge(s["V"], m + 2)
                pe.wait_ge(s["am"], m + 1)
                for c in range(2):
                    for u in range(P // D):
                        g, j = u // 4, u % 4
                        mm(OG[c * C:(c + 1) * C, u * 32:(u + 1) * 32], Am[:, 2 * g + c, j, :],
                           Vbd[par][:, 8 * c + u, :], u == 0, False)

            def attend_state(m, par):
                for c in range(2):
                    pe.wait_ge(s[f"T{c}"], m + 1)
                    for g in range(KC):
                        last = mm(OG[c * C:(c + 1) * C, g * P:(g + 1) * P], Qh[par][:, g, c * C:(c + 1) * C],
                                  Tst[c][:, g, :], False)
                last.then_inc(s["og"], 1)

            def logits(m, par):
                pe.wait_ge(s["x1T"], m + 1)
                if alive(m - 1, NT):
                    pe.wait_ge(s["lg"], m)
                for c in range(KC):
                    last = mm(X7[:, HID:HID + E], x1T[:, c, :], gwT[:, c, :], c == 0, c == KC - 1)
                last.then_inc(s["lgp"], 1)

            def shared_in(m, halves):
                par = m % 2
                if 0 in halves:
                    pe.wait_ge(s["x1Tc"], m + 1)
                    if m == 0:
                        pe.wait_ge(s["Kt"], NT)
                    elif m == 1:
                        pe.wait_ge(s["sgt"], NT)
                    elif m == LATE.start:
                        pe.wait_ge(s["hT"], NP)
                        pe.wait_ge(s["xt"], NP)
                    if m >= 2:
                        pe.wait_ge(s["shh"], m - 1)
                for a in halves:
                    for n in range(2):
                        for c in range(KC):
                            last = mm(SHb[par][0:I, (2 * a + n) * P:(2 * a + n + 1) * P], sT[n][:, c, a * I:(a + 1) * I],
                                      x1T_all[:, m, c * P:(c + 1) * P], c == 0, c == KC - 1)
                if SM - 1 in halves:
                    last.then_inc(s["sgp"], 1)

            def shared_step(m, gate_up, down_prev):
                par = m % 2
                if gate_up:
                    shared_in(m, range(SM))
                if down_prev:
                    pe.wait_ge(s["shh"], m)
                    if m == 1:
                        pe.wait_ge(s["am"], NT)
                    if m >= 3:
                        pe.wait_ge(s["base"], m - 2)
                    for a in range(SM):
                        last = mm(SDb[1 - par], sh_h[1 - par][:, a, :], sdT[:, a, :], a == 0, a == SM - 1)
                    last.then_inc(s["sdp"], 1)

            def tile_step(i, par):
                now, nxt, prev = alive(i, NT), alive(i + 1, NT), alive(i - 1, NT)
                start, end = isinstance(i, int) and i == -1, isinstance(i, int) and i >= NT - 1
                if now:
                    state(i, par)
                if nxt and not start:
                    values(i + 1, 1 - par)
                if prev:
                    out_proj(i - 1, 1 - par)
                if nxt:
                    queries_keys(i + 1, 1 - par)
                if start:
                    values(i + 1, 1 - par)
                if alive(i + 2, NT):
                    t_x(i + 2, par)
                if start:
                    t_weights()
                    t_k(i + 1, 1 - par)
                    scores(i + 1, 1 - par)
                if now:
                    attend(i, par)
                    attend_state(i, par)
                if end and i == NT - 1:
                    shared_in(0, range(0, SM - 1))
                if alive(i - 2, NT):
                    count(i - 2, par)
                if end and i == NT - 1:
                    shared_in(0, range(SM - 1, SM))
                if end and i == NT:
                    shared_in(1, range(SM))
                if prev:
                    t_x1(i - 1, 1 - par)
                if alive(i + 2, NT):
                    low_rank(i + 2, par)
                    output_gate(i + 2, par)
                if nxt and not start:
                    scores(i + 1, 1 - par)
                if alive(i + 2, NT):
                    decay_in(i + 2, par)
                if nxt and not start:
                    t_k(i + 1, 1 - par)
                if prev and end:
                    logits(i - 1, 1 - par)
                if now:
                    t_o(i, par)
                if prev and not end:
                    logits(i - 1, 1 - par)
            run_tiles(pe, tile_step)
            for m in range(EARLY.start + 1, EARLY.stop + 1):
                shared_step(m, 1 < m < EARLY.stop, True)

            def pair_step(p, k, h):
                if alive(p, NP):
                    pe.wait_ge(d_gx[k % GXR], slot_loads(k, h))
                    if alive(p - 2, NP):
                        pe.wait_ge(s["xt"], p - 1)
                    elif p == 1:
                        pe.wait_ge(s["shh"], EARLY.stop)
                    for c in range(KC):
                        last = pe.transpose(XTb[k % 2][:, c * P:(c + 1) * P], gx[:, k % GXR, c * P:(c + 1) * P], ident)
                    last.then_inc(s["xtp"], 1)
                if alive(p - 2, NP):
                    if k == 2:
                        pe.wait_ge(s["base"], EARLY.stop)
                    pe.wait_ge(s["hid"], p - 1)
                    pe.transpose(HTb[k % 2][0:I, 0:P], hid[:, k % 2, :], ident).then_inc(s["hTp"], 1)
                if alive(p - 1, NP):
                    q, r = (k - 1) % 2, weight_place(k - 1)
                    pe.wait_ge(d_w[r], weight_loads(k - 1, h))
                    pe.wait_ge(s["xt"], p)
                    if alive(p - 3, NP):
                        pe.wait_ge(s["hid"], p - 2)
                    for c in range(KC):
                        for e in range(2):
                            last = mm(GUb[q][e * CAP:(e + 1) * CAP, 0:2 * I], gxT[:, q, c * P + e * CAP:c * P + (e + 1) * CAP],
                                      wgu_r[:, r, 2 * e + c, :], c == 0, c == KC - 1)
                    last.then_inc(s["gu"], 1)
                if alive(p - 2, NP):
                    q, r = k % 2, weight_place(k - 2)
                    pe.wait_ge(s["hT"], p - 1)
                    if alive(p - 4, NP):
                        pe.wait_ge(s["ev"], p - 3)
                    for e in range(2):
                        last = mm(DNb[q][e * CAP:(e + 1) * CAP, 0:HID], hidT[:, q, e * CAP:(e + 1) * CAP],
                                  wdn_r[0:I, r, e, :], True)
                    last.then_inc(s["dn"], 1)
            run_pairs(pe, pair_step)
            run_shared(pe, shared_step, LATE)

            for m in range(NT):
                pe.wait_ge(s["hsum"], m + 1)
                if m >= 4:
                    pe.wait_ge(s["res"], m - 3)
                else:
                    pe.wait_ge(s["base"], NT)
                for k in range(K // 2):
                    mm(CSb[m % 4][:, 0:HID], ident, half_sum[m % 2][:, k * HID:(k + 1) * HID], k == 0, False)
                mm(CSb[m % 4][:, 0:HID], ident, base[:, m, :], False).then_inc(s["csp"], 1)

        @block.scalar
        def _(act):
            act.preload_act_table_set("natural_log_exp_and_others")

            def copy(o, i):
                return act.activation(o, i, ACT.Copy)

            def gate_in(m, par):
                act.wait_ge(s["og"], m + 1)
                act.activation(sq[:, :], OG[:, 0:HID], ACT.Square).then_inc(s["sq"], 1)

            def rms(m, par):
                act.wait_ge(s["ms"], m + 1)
                act.activation(ms_ln[:, :], ms[:, :], ACT.Ln, bias=eps_col, scale=1.0 / D).then_inc(s["msl"], 1)
                act.wait_ge(s["msl"], m + 1)
                act.activation(rs[:, :], ms_ln[:, :], ACT.Exp, scale=-0.5).then_inc(s["rs"], 1)

            def ev_x(m, par):
                act.wait_ge(s["xTp"], m + 1)
                copy(xT[:, :, :].rearrange("p c t -> p (c t)"), tA[:, 0:256])
                copy(xTd[:, :, :, :], tA[:, 0:256].rearrange("p (u t) -> p u t", t=C).unsqueeze(2)
                     .to_broadcast([P, KC * 2, 2, C])).then_inc(s["xT"], 1)

            def ev_k(m, par):
                act.wait_ge(s["khTp"], m + 1)
                copy(Kt[:, :], QK[:, 0:HID]).then_inc(s["Kt"], 1)

            def ev_o(m, par):
                act.wait_ge(s["oTp"], m + 1)
                copy(oT[:, :, :].rearrange("p c t -> p (c t)"), tA[:, 256:512]).then_inc(s["oT"], 1)

            def ev_low(m, par):
                act.wait_ge(s["lowp"], m + 1)
                if first(m):
                    act.wait_ge(s["low1"], 1)
                copy(low[0:LOWR, :], QK[0:LOWR, HID:HID + P]).then_inc(s["low"], 1)

            def ev_v(m, par):
                act.wait_ge(s["Vp"], m + 1)
                v = VO[:, :].rearrange("p (u n) -> p u n", n=2 * D)
                for h in range(2):
                    copy(Vbd[par][h * C:(h + 1) * C, :, h * D:(h + 1) * D], v[h * C:(h + 1) * C, :, h * D:(h + 1) * D])
                for c in range(2):
                    last = copy(Vz[par][c * C:(c + 1) * C, c, :], VO[c * C:(c + 1) * C, c * HID:(c + 1) * HID])
                last.then_inc(s["V"], 1)

            def soft(m, par):
                act.wait_ge(s["zp"], m + 1)
                act.activation(z_abs[:, :], tB[:, :], ACT.Abs).then_inc(s["absd"], 1)
                act.wait_ge(s["absd"], m + 1)
                act.activation(z_exp[:, :], z_abs[:, :], ACT.Exp, scale=-1.0).then_inc(s["expd"], 1)
                act.wait_ge(s["expd"], m + 1)
                if alive(m - 1, NT):
                    act.wait_ge(s["gk"], m)
                if first(m):
                    act.wait_ge(s["cst"], 16)
                act.activation(z_ln[:, :], z_exp[:, :], ACT.Ln, bias=ones[:, 0:1]).then_inc(s["lnd"], 1)

            def ln_std(m, par):
                act.wait_ge(s["mv"], m + 1)
                act.activation(dev2[:, :], y[:, :], ACT.Square, bias=nmean[:, :], accum_out=vsum[:, :]).then_inc(s["vs"], 1)
                act.wait_ge(s["vs"], m + 1)
                act.activation(v_ln[:, :], vsum[:, :], ACT.Ln, bias=eps_col, scale=1.0 / HID).then_inc(s["vl"], 1)
                act.wait_ge(s["vl"], m + 1)
                act.activation(rstd[:, :], v_ln[:, :], ACT.Exp, scale=-0.5).then_inc(s["rst"], 1)

            def decays(m, par):
                act.wait_ge(s["gk"], m + 1)
                if first(m):
                    act.wait_ge(s["pre"], 10)
                act.activation(sigm[:, :], lsg[:, HID:2 * HID], ACT.Exp).then_inc(s["sigm"], 1)
                act.wait_ge(s["Dc"], m + 1)
                d = Dc[:, :, :].rearrange("p u s -> p (u s)")
                act.activation(EQ[:, :], d, ACT.Exp, scale=1.0 / GLN)
                act.activation(EK[:, :], d, ACT.Exp, scale=-1.0 / GLN).then_inc(s["ex"], 1)
                if alive(m - 1, NT):
                    act.wait_ge(s["fc"], 2 * m)
                act.activation(fa[par][:, :], gk[:, :, 0], ACT.Exp, scale=1.0 / GLN)
                act.activation(fb[par][:, :], Dc[:, :, C - 1], ACT.Exp, scale=1.0 / GLN).then_inc(s["ab"], 1)

            def ev_x1(m, par):
                act.wait_ge(s["x1Tp"], m + 1)
                if alive(m - 1, NT):
                    act.wait_ge(s["x1Tc"], m)
                copy(x1T[:, :, :].rearrange("p c t -> p (c t)"), X7[:, 0:256]).then_inc(s["x1T"], 1)

            def keep_x1(m, par):
                act.wait_ge(s["x1"], m + 1)
                act.nop(nofuse=True)
                copy(x1_all[:, bass.ds(m, 1), :].rearrange("p a h -> p (a h)"), x1s[par][:, :]).then_inc(s["x1c"], 1)

            def keep_x1T(m, par):
                act.wait_ge(s["x1T"], m + 1)
                act.nop(nofuse=True)
                copy(x1T_all[:, bass.ds(m, 1), :].rearrange("p a h -> p (a h)"),
                     x1T[:, :, :].rearrange("p c t -> p (c t)")).then_inc(s["x1Tc"], 1)

            def fill_rows(m, par):
                act.wait_ge(s["x1c"], m + 1)
                if alive(m - 2, NT):
                    act.wait_ge(d_scat[par], half(m - 2, par, K * 16))
                act.nop(nofuse=True)
                copy(rows[par][:, 0:HID], x1_all[:, bass.ds(m, 1), :].rearrange("p a h -> p (a h)")).then_inc(s["xrow"], 1)

            def ev_logits(m, par):
                act.wait_ge(s["lgp"], m + 1)
                copy(lg[:, :], X7[:, HID:HID + E]).then_inc(s["lg"], 1)

            def spread_q(m, par):
                act.wait_ge(s["qh"], m + 1)
                for j in range(4):
                    r = slice(32 * j, 32 * j + 32)
                    last = copy(Qbd[r, :, j, :], Qh[par][r, :, :].rearrange("p g (c t) -> p (g c) t", c=2))
                last.then_inc(s["qbd"], 1)

            def softmax(m, par):
                act.wait_ge(s["nmx"], m + 1)
                act.activation(e64[:, :], lg[:, :], ACT.Exp, bias=nmx[:, :], accum_out=esum[:, :])
                act.activation(e8[:, :], mx8[:, :], ACT.Exp, bias=nmx[:, :]).then_inc(s["es"], 1)

            def tile_step(i, par):
                now, nxt, prev = alive(i, NT), alive(i + 1, NT), alive(i - 1, NT)
                last, end = isinstance(i, int) and i == NT - 1, isinstance(i, int) and i >= NT
                if prev and not end:
                    ev_o(i - 1, 1 - par)
                if alive(i - 2, NT) and not (end and i == NT):
                    ev_logits(i - 2, par)
                start = isinstance(i, int) and i == -1
                if nxt:
                    soft(i + 1, 1 - par)
                    if not start:
                        ev_v(i + 1, 1 - par)
                    decays(i + 1, 1 - par)
                if last or end:
                    fill_rows(i - 2, par)
                if last:
                    gate_in(i, par)
                if end:
                    softmax(i - 2, par)
                if prev:
                    ln_std(i - 1, 1 - par)
                if start:
                    spread_q(i + 1, 1 - par)
                    ev_k(i + 1, 1 - par)
                if alive(i + 2, NT):
                    ev_x(i + 2, par)
                if alive(i - 2, NT) and not end:
                    softmax(i - 2, par)
                if last:
                    rms(i, par)
                    ev_x1(i - 1, 1 - par)
                    ev_logits(i - 1, 1 - par)
                    ev_o(i, par)
                if nxt and not start:
                    spread_q(i + 1, 1 - par)
                if now and not last:
                    gate_in(i, par)
                if start:
                    ev_v(i + 1, 1 - par)
                if alive(i + 2, NT):
                    ev_low(i + 2, par)
                if now and not last:
                    rms(i, par)
                if alive(i - 2, NT) and not (last or end):
                    fill_rows(i - 2, par)
                if prev and end:
                    ev_x1(i - 1, 1 - par)
                if prev:
                    keep_x1(i - 1, 1 - par)
                    if not last and not end:
                        ev_x1(i - 1, 1 - par)
                if nxt and not start:
                    ev_k(i + 1, 1 - par)
                if prev:
                    keep_x1T(i - 1, 1 - par)
            run_tiles(act, tile_step)

            def shared_step(m, gate_up, down_prev):
                if gate_up:
                    par = m % 2
                    act.wait_ge(s["sgp"], m + 1)
                    if m >= 2:
                        act.wait_ge(s["shh"], m - 1)
                    g = SHb[par][0:I, :].rearrange("p (a n t) -> p a n t", a=SM, n=2)
                    act.activation(sh_g[par][:, :, :], g[:, :, 0, :], ACT.Silu).then_inc(s["sil"], 1)
            run_shared(act, shared_step, EARLY)

            def pair_step(p, k, h):
                if alive(p, NP):
                    act.wait_ge(s["xtp"], p + 1)
                    if alive(p - 2, NP):
                        act.wait_ge(s["gu"], p - 1)
                    copy(gxT[:, k % 2, :], XTb[k % 2][:, 0:HID]).then_inc(s["xt"], 1)
                if alive(p - 1, NP):
                    q = (k - 1) % 2
                    act.wait_ge(s["gu"], p)
                    if alive(p - 3, NP):
                        act.wait_ge(s["hid"], p - 2)
                    act.activation(sg[:, q, :], GUb[q][:, 0:I], ACT.Silu).then_inc(s["sig"], 1)
                if alive(p - 2, NP):
                    q, r = k % 2, (k - 2) % GXR
                    act.wait_ge(s["dn"], p - 1)
                    act.wait_ge(s["wd"], p - 1)
                    act.wait_ge(d_put[r], put_done(k - 2 - GXR, h))
                    act.activation(eo[r][:, :], DNb[q][:, 0:HID], ACT.Copy, scale=wsel[:, r:r + 1]).then_inc(s["ev"], 1)
            run_pairs(act, pair_step)
            run_shared(act, shared_step, LATE)

            act.preload_act_table_set("natural_log_exp_and_others")

            def final_std(m):
                act.wait_ge(s["mvf"], m + 1)
                act.activation(vf_ln[:, :], mvf[:, 1:2], ACT.Ln, bias=eps_col).then_inc(s["vfl"], 1)
                act.wait_ge(s["vfl"], m + 1)
                act.activation(rstdf[:, :], vf_ln[:, :], ACT.Exp, scale=-0.5).then_inc(s["rsf"], 1)
            with act.Fori(0, NT) as m:
                final_std(m)

        @block.vector
        def _(dve):
            dve.wait_ge(s["cst"], 16)
            dve.wait_ge(s["pre"], 10)

            def keep_weights():
                dve.wait_ge(s["rawT"], 1)
                dve.tensor_copy(gwT[:, :, :].rearrange("p c e -> p (c e)"), SCb[:, 0, 0:KC * E]).then_inc(s["rawE"], 1)
                for n, bank in enumerate((SCb[:, 1, :], PX)):
                    dve.tensor_copy(sT[n][:, :, :].rearrange("p c i -> p (c i)"), bank[:, 0:KC * SI]).then_inc(s["rawE"], 1)
                dve.tensor_copy(sdT[:, :, :].rearrange("p m h -> p (m h)"), X7[0:I, :]).then_inc(s["rawE"], 1)

            def scale_wo():
                dve.wait_ge(s["w_out"], 16)
                dve.wait_ge(s["nw"], 16 * (P // D))
                for c in range(KC):
                    dve.tensor_scalar(wo[:, c, :], wo[:, c, :], nw_col[:, 0:1], None, ALU.mult).then_inc(s["wo_ready"], 1)

            def squares(m, par):
                dve.wait_ge(s["sq"], m + 1)
                dve.tensor_reduce(ms[:, :], sq[:, :].rearrange("p (h d) -> p h d", d=D), AX.X, ALU.add).then_inc(s["ms"], 1)

            def gated(m, par):
                dve.wait_ge(s["rs"], m + 1)
                dve.tensor_tensor(on[:, :].rearrange("p (h d) -> p h d", d=D),
                                  OG[:, 0:HID].rearrange("p (h d) -> p h d", d=D),
                                  rs[:, :].unsqueeze(2).to_broadcast([P, H, D]), ALU.mult).then_inc(s["on"], 1)
                dve.wait_ge(s["on"], m + 1)
                dve.tensor_tensor(of[:, :], on[:, :], sgate[par][:, :], ALU.mult).then_inc(s["of"], 1)

            def causal(m, par):
                dve.wait_ge(s["sc"], m + 1)
                dve.nop(nofuse=True)
                dve.copy_predicated(Am[:, :, :, :], caus.unsqueeze(1).unsqueeze(1).to_broadcast([P, 4, 4, C]),
                                    SC[:, :, :].rearrange("p u (j t) -> p u j t", t=C)).then_inc(s["am"], 1)

            def post_sum(m, par):
                if first(m):
                    dve.wait_ge(s["xall"], 16)
                dve.wait_ge(s["Wop"], m + 1)
                dve.scalar_tensor_tensor(y[:, :], tA[:, 0:HID], 1.0, x_all[:, bass.ds(m, 1), :].rearrange("p a h -> p (a h)"),
                                         ALU.mult, ALU.add, accum_out=ysum[:, :]).then_inc(s["y"], 1)

            def post_mean(m, par):
                dve.wait_ge(s["y"], m + 1)
                dve.tensor_scalar(nmean[:, :], ysum[:, :], -1.0 / HID, None, ALU.mult).then_inc(s["mv"], 1)

            def post_norm(m, par):
                dve.wait_ge(s["rst"], m + 1)
                if alive(m - 2, NT):
                    dve.wait_ge(s["x1c"], m - 1)
                dve.tensor_scalar(x1s[par][:, :], y[:, :], nmean[:, :], rstd[:, :], ALU.add, ALU.mult)\
                    .then_inc(s["x1"], 1)

            def queried_state(m, par, c):
                slot = m + m // TPB
                src = Umid[:, :, :] if c else Sst[:, bass.ds(slot, 1), :].rearrange("p a (g n) -> p (a g) n", g=KC)
                if c:
                    dve.wait_ge(s["U"], 2 * m + 1)
                else:
                    dve.wait_ge(s["fc"], 2 * m + 2)
                    if alive(m - 1, NT):
                        dve.wait_ge(s["U"], 2 * m)
                        dve.wait_ge(s["og"], m)
                for g in range(KC):
                    last = dve.scalar_tensor_tensor(Tst[c][:, g, :], src[:, g, :], fc[par][:, c, g:g + 1], blk,
                                                    ALU.mult, ALU.mult)
                last.then_inc(s[f"T{c}"], 1)

            def closing_state(m, par, c):
                slot = m + m // TPB + 1
                dst = Sst[:, bass.ds(slot, 1), :].rearrange("p a (g n) -> p (a g) n", g=KC) if c else Umid[:, :, :]
                dve.wait_ge(s[f"T{c}"], m + 1)
                dve.wait_ge(s["Pp"], m + 1)
                dve.tensor_tensor(dst, PX[:, :].rearrange("p (g c n) -> p g c n", g=KC, c=2)[:, :, c, :],
                                  Tst[c][:, :, :], ALU.add).then_inc(s["U"], 1)

            def log_sigmoid(m, par):
                dve.wait_ge(s["lnd"], m + 1)
                dve.scalar_tensor_tensor(lsg[:, :], tB[:, :], 0.0, z_ln[:, :], ALU.min, ALU.subtract).then_inc(s["gk"], 1)

            def decay(m, par):
                dve.wait_ge(s["gk"], m + 1)
                dve.tensor_tensor_scan(Dc[:, :, :].rearrange("p u s -> p (u s)"), lsg[:, 0:HID], scan_keep, 0.0,
                                       ALU.add, ALU.mult).then_inc(s["Dc"], 1)

            def silu_gate(m, par):
                dve.wait_ge(s["sigm"], m + 1)
                dve.tensor_tensor(sgate[par][:, :], tB[:, HID:2 * HID], sigm[:, :], ALU.mult).then_inc(s["sgt"], 1)

            def decayed(m, par):
                dve.wait_ge(s["qk"], m + 1)
                dve.wait_ge(s["ex"], m + 1)
                dve.tensor_tensor(Kh[:, :, :].rearrange("p g t -> p (g t)"), QK[:, HID:2 * HID], EK[:, :], ALU.mult)\
                    .then_inc(s["kh"], 1)
                dve.scalar_tensor_tensor(Qh[par][:, :, :].rearrange("p g t -> p (g t)"), QK[:, 0:HID], D ** -0.5,
                                         EQ[:, :], ALU.mult, ALU.mult).then_inc(s["qh"], 1)
                dve.wait_ge(s["kh"], m + 1)
                for h in range(2):
                    last = dve.tensor_scalar(Kbd[:, :, h, :], Kh[:, :, :].rearrange("p g (c t) -> p (g c) t", c=2),
                                             cst[:, C_PAR + h:C_PAR + h + 1], None, ALU.mult)
                last.then_inc(s["kbd"], 1)
            def top8(m, par):
                dve.wait_ge(s["lg"], m + 1)
                dve.nop(nofuse=True)
                dve.max(mx8[:, :], lg[:, :]).then_inc(s["mx"], 1)

            def top8_index(m, par):
                dve.wait_ge(s["mx"], m + 1)
                dve.tensor_scalar(nmx[:, :], mx8[:, 0:1], -1.0, None, ALU.mult).then_inc(s["nmx"], 1)
                dve.max_index(ix8[:, :], mx8[:, :], lg[:, :]).then_inc(s["ix"], 1)

            def index_as_float(m, par):
                dve.wait_ge(s["ix"], m + 1)
                dve.tensor_copy(idx_f[:, :], ix8[:, 0:K]).then_inc(s["idx"], 1)

            def one_hot(m, par):
                dve.wait_ge(s["idx"], m + 1)
                dve.tensor_tensor(oh[:, :, :], eiota.unsqueeze(1).to_broadcast([P, K, E]),
                                  idx_f[:, :].unsqueeze(2).to_broadcast([P, K, E]), ALU.is_equal).then_inc(s["oh"], 1)

            def selection(m, par):
                dve.wait_ge(s["oh"], m + 1)
                dve.tensor_reduce(sel[:, :], oh[:, :, :].rearrange("p k e -> p e k"), AX.X, ALU.add).then_inc(s["sel"], 1)

            def place(m, par):
                dve.wait_ge(s["es"], m + 1)
                dve.reciprocal(erec[:, :], esum[:, :]).then_inc(s["rec"], 1)
                dve.wait_ge(s["cum"], m + 1)
                dve.tensor_tensor(pm[:, :, :], PX[:, 0:E].unsqueeze(1).to_broadcast([P, K, E]), oh[:, :, :],
                                  ALU.mult).then_inc(s["pm"], 1)
                dve.tensor_tensor(sel_acc[:, :], sel_acc[:, :], sel[:, :], ALU.add).then_inc(s["acc"], 1)
                dve.wait_ge(s["rec"], m + 1)
                if alive(m - 2, NT):
                    dve.wait_ge(d_scat[par], half(m - 2, par, K * 16))
                dve.tensor_scalar(rows[par][:, WCOL:WCOL + K], e8[:, 0:K], erec[:, :], None, ALU.mult)
                dve.tensor_copy(rows[par][:, ICOL:ICOL + K], idx_f[:, :])
                dve.tensor_copy(rows[par][:, DCOL:DCOL + K], cst[:, bass.ds(C_D + m * K, K)]).then_inc(s["wr"], 1)
                dve.wait_ge(s["pm"], m + 1)
                dve.tensor_reduce(pos[:, :], pm[:, :, :], AX.X, ALU.add).then_inc(s["pos"], 1)

            def place_end(m, par):
                dve.wait_ge(s["pos"], m + 1)
                dve.tensor_scalar(over[:, :], pos[:, :], CAP - 0.5, float(NOWHERE), ALU.is_ge, ALU.mult)
                dve.scalar_tensor_tensor(slot_f[:, :], idx_f[:, :], float(CAP), pos[:, :], ALU.mult, ALU.add).then_inc(s["sf"], 1)
                dve.wait_ge(s["sf"], m + 1)
                dve.tensor_tensor(slot_u[par][:, :], slot_f[:, :], over[:, :], ALU.add).then_inc(s["slot"], 1)

            def shared_hidden(m):
                par = m % 2
                dve.wait_ge(s["sil"], m + 1)
                if m >= 2:
                    dve.wait_ge(s["sdp"], m - 1)
                u = SHb[par][0:I, :].rearrange("p (a n t) -> p a n t", a=SM, n=2)
                dve.tensor_tensor(sh_h[par][:, :, :], sh_g[par][:, :, :], u[:, :, 1, :], ALU.mult).then_inc(s["shh"], 1)

            def shared_step(m, gate_up, down_prev):
                if gate_up and m >= 2:
                    shared_hidden(m)
                if down_prev:
                    dve.wait_ge(s["sdp"], m)
                    dve.wait_ge(s["xrow"], m)
                    dve.tensor_tensor(base[:, m - 1, :], x1_all[:, m - 1, :], SDb[(m - 1) % 2], ALU.add).then_inc(s["base"], 1)

            def tile_step(i, par):
                now, nxt, prev = alive(i, NT), alive(i + 1, NT), alive(i - 1, NT)
                late = alive(i - 2, NT)
                start, last, after, done = (isinstance(i, int) and i == n for n in (-1, NT - 1, NT, NT + 1))
                if now:
                    queried_state(i, par, 0)
                if late:
                    top8(i - 2, par)
                if now:
                    closing_state(i, par, 0)
                if late:
                    top8_index(i - 2, par)
                if now:
                    queried_state(i, par, 1)
                if late:
                    index_as_float(i - 2, par)
                if now:
                    closing_state(i, par, 1)
                if last:
                    post_sum(i - 1, 1 - par)
                if nxt:
                    log_sigmoid(i + 1, 1 - par)
                if late:
                    one_hot(i - 2, par)
                if last:
                    post_mean(i - 1, 1 - par)
                if nxt:
                    decay(i + 1, 1 - par)
                if late:
                    selection(i - 2, par)
                if done:
                    shared_hidden(0)
                    shared_hidden(1)
                if prev and not last:
                    post_sum(i - 1, 1 - par)
                    post_mean(i - 1, 1 - par)
                if nxt:
                    silu_gate(i + 1, 1 - par)
                    decayed(i + 1, 1 - par)
                if start:
                    keep_weights()
                if last:
                    squares(i, par)
                if prev and not after:
                    post_norm(i - 1, 1 - par)
                if late:
                    place(i - 2, par)
                if now and not last:
                    squares(i, par)
                if after:
                    post_norm(i - 1, 1 - par)
                if late:
                    place_end(i - 2, par)
                if now:
                    gated(i, par)
                if nxt:
                    causal(i + 1, 1 - par)
                if start:
                    scale_wo()
            run_tiles(dve, tile_step)
            run_shared(dve, shared_step, EARLY)

            def pair_step(p, k, h):
                if alive(p - 2, NP):
                    dve.wait_ge(s["hTp"], p - 1)
                    if alive(p - 4, NP):
                        dve.wait_ge(s["dn"], p - 3)
                    dve.tensor_copy(hidT[:, k % 2, :], HTb[k % 2][0:I, 0:P]).then_inc(s["hT"], 1)
                if alive(p - 1, NP):
                    q = (k - 1) % 2
                    dve.wait_ge(s["sig"], p)
                    dve.tensor_tensor(hid[:, q, :], sg[:, q, :], GUb[q][:, I:2 * I], ALU.mult).then_inc(s["hid"], 1)
                if alive(p, NP):
                    r = k % GXR
                    dve.wait_ge(d_gx[r], slot_loads(k, h))
                    dve.wait_ge(d_put[r], put_done(k - GXR, h))
                    ecol = cst[:, bass.ds(C_ECOL + p, 1)]
                    dve.scalar_tensor_tensor(junk[:, :], gx[:, r, ICOL:ICOL + K], ecol, gx[:, r, WCOL:WCOL + K],
                                             ALU.is_equal, ALU.mult, accum_out=wsel[:, r:r + 1]).then_inc(s["wd"], 1)
                    dve.wait_ge(s["wd"], p + 1)
                    dve.scalar_tensor_tensor(junk[:, :], gx[:, r, ICOL:ICOL + K], ecol, gx[:, r, DCOL:DCOL + K],
                                             ALU.is_equal, ALU.mult, accum_out=dsel[:, r:r + 1]).then_inc(s["dsel"], 1)
                    dve.wait_ge(s["dsel"], p + 1)
                    dve.tensor_scalar(dest[r][:, :], dsel[:, r:r + 1], float(NOWHERE), None, ALU.add).then_inc(s["dest"], 1)
            run_pairs(dve, pair_step)
            run_shared(dve, shared_step, LATE)

            def halves(m):
                dve.wait_ge(d_cin[m], 16)
                if m >= 2:
                    dve.wait_ge(s["csp"], m - 1)
                dve.tensor_tensor(half_sum[m % 2][:, :], cin[m][:, 0:K // 2 * HID], cin[m][:, K // 2 * HID:K * HID], ALU.add)\
                    .then_inc(s["hsum"], 1)

            def stats(m):
                dve.wait_ge(s["csp"], m + 1)
                dve.bn_stats(bnf[:, :], CSb[m % 4][:, 0:HID]).then_inc(s["bnf"], 1)
                dve.wait_ge(s["bnf"], m + 1)
                dve.bn_aggr(mvf[:, :], bnf[:, :]).then_inc(s["mvf"], 1)

            def norm(m):
                dve.wait_ge(s["rsf"], m + 1)
                dve.tensor_scalar(res[m], CSb[m % 4][:, 0:HID], mvf[:, 0:1], rstdf[:, :], ALU.subtract, ALU.mult)\
                    .then_inc(s["res"], 1)
            halves(0)
            halves(1)
            for m in range(NT):
                stats(m)
                if m + 2 < NT:
                    halves(m + 2)
                norm(m)



_INS = ["L0_attn_x", "L0_attn_Wq", "L0_attn_Wk", "L0_attn_Wv", "L0_attn_Wg1", "L0_attn_Wg2", "L0_attn_bg2",
        "L0_attn_Wgate", "L0_attn_norm_w", "L0_attn_Wo", "L0_ffn_gate_w", "L0_ffn_gate_up_proj", "L0_ffn_down_proj",
        "L0_ffn_shared_gate_w", "L0_ffn_shared_up_w", "L0_ffn_shared_down_w"]


def kernel(**inputs):
    import concourse.bacc as bacc
    from concourse.bass_utils import run_bass_kernel_spmd

    nc = bacc.Bacc("TRN2", target_bir_lowering=False, num_devices=1)
    arrays = {"consts": constants()}
    args = [nc.dram_tensor("consts", arrays["consts"].shape, F32, kind="ExternalInput").ap()]
    for name in _INS:
        a = np.ascontiguousarray(inputs[name])
        arrays[f"in_{name}"] = a
        args.append(nc.dram_tensor(f"in_{name}", a.shape, mybir.dt.from_np(a.dtype), kind="ExternalInput").ap())
    args.append(nc.dram_tensor("result", (B, L, HID), F32, kind="ExternalOutput").ap())
    build(nc, *args)
    r = run_bass_kernel_spmd(nc, [arrays], core_ids=[0])
    return r.results[0]["result"]
```
